# Optimizing a Trainium2 kernel written in Bass

```python
import numpy as np
import jax
import jax.numpy as jnp

def _softmax(x, axis=-1):
    return jax.nn.softmax(x, axis=axis)

def _gelu(x):
    return jax.nn.gelu(x, approximate=True)

def _silu(x):
    return jax.nn.silu(x)

def _sigmoid(x):
    return jax.nn.sigmoid(x)

def _layernorm(x, axis=-1, eps=1e-05):
    m = jnp.mean(x, axis=axis, keepdims=True)
    v = jnp.var(x, axis=axis, keepdims=True)
    return (x - m) / jnp.sqrt(v + eps)

def _scatter_add(tgt, idx, src, axis=0):
    return tgt.at[idx].add(src)

def _segment_sum(src, seg, n):
    return jax.ops.segment_sum(src, seg, n)
kernel_name = 'mk_vit_tower_d1_tok_img512_r4_b161ea'

def setup_inputs(seed: int=0):
    np.random.seed(seed)
    _w = jnp.asarray

    def _rec_inputs():
        import jax
        import jax.numpy as jnp
        _rk = jax.random.key(seed)
        x = -0.000356955 + 1 * jax.random.normal(jax.random.fold_in(_rk, 1), (16, 3, 112, 112), jnp.float32)
        return x
    x = _rec_inputs()

    def _L0_tok_setup():
        import jax, jax.numpy as jnp
        import numpy as np
        IMG = 112
        P = 16
        C = 3
        D = 128
        DC = 8
        DS = 4
        NH = IMG // P
        NPATCH = NH * NH
        PDIM = C * P * P
        BATCH = 32
        EPS = 1e-05
        key = jax.random.key(seed)
        ks = jax.random.split(key, 10)

        def lin(k, fan_in, shape):
            bound = 1.0 / np.sqrt(fan_in)
            return jax.random.uniform(k, shape, jnp.float32, -bound, bound)
        return {'images': jax.random.normal(ks[0], (BATCH, C, IMG, IMG), jnp.float32), 'W_patch': lin(ks[1], PDIM, (PDIM, D)), 'b_patch': jnp.zeros((D,), jnp.float32), 'pos_embed': jax.random.normal(ks[2], (1, NPATCH, D), jnp.float32) * 0.02, 'W_coord': lin(ks[3], D, (D, DC)), 'b_coord': jnp.zeros((DC,), jnp.float32), 'W_spinor': lin(ks[4], D, (D, DS)), 'b_spinor': jnp.zeros((DS,), jnp.float32), 'W_embed': lin(ks[5], DC, (DC, D)), 'b_embed': jnp.zeros((D,), jnp.float32), 'ln_gamma': jnp.ones((D,), jnp.float32), 'ln_beta': jnp.zeros((D,), jnp.float32), 'W_out': lin(ks[6], D, (D, D)), 'b_out': jnp.zeros((D,), jnp.float32)}
    _L0_tok_all = _L0_tok_setup()
    _L0_tok_in = {k: v for k, v in _L0_tok_all.items() if k in ('W_patch', 'b_patch', 'pos_embed', 'W_coord', 'b_coord', 'W_spinor', 'b_spinor', 'W_embed', 'b_embed', 'ln_gamma', 'ln_beta', 'W_out', 'b_out')}
    del _L0_tok_all

    def _L0_attn_setup():
        import jax, jax.numpy as jnp
        import numpy as np
        B, T, D, H = (2, 512, 128, 8)
        HD = D // H
        EPS = 1e-05
        key = jax.random.key(seed)
        ks = jax.random.split(key, 8)
        s = 1.0 / np.sqrt(D)
        return {'x': jax.random.normal(ks[0], (B, T, D), dtype=jnp.float32), 'Wq': jax.random.uniform(ks[1], (D, D), jnp.float32, -s, s), 'bq': jnp.zeros((D,), jnp.float32), 'Wk': jax.random.uniform(ks[2], (D, D), jnp.float32, -s, s), 'bk': jnp.zeros((D,), jnp.float32), 'Wv': jax.random.uniform(ks[3], (D, D), jnp.float32, -s, s), 'bv': jnp.zeros((D,), jnp.float32), 'gn_w': jnp.ones((D,), jnp.float32), 'gn_b': jnp.zeros((D,), jnp.float32), 'gamma': jnp.float32(0.9)}
    _L0_attn_all = _L0_attn_setup()
    _L0_attn_in = {k: v for k, v in _L0_attn_all.items() if k in ('Wq', 'bq', 'Wk', 'bk', 'Wv', 'bv', 'gn_w', 'gn_b', 'gamma')}
    del _L0_attn_all

    def _L0_ffn_setup():
        import jax, jax.numpy as jnp
        import numpy as np
        E = 64
        K = 6
        NS = 2
        D = 128
        F = 128

        def _swiglu_ffn(x, wg, wu, wd):
            return jax.nn.silu(x @ wg) * (x @ wu) @ wd
        key = jax.random.key(seed)
        ks = jax.random.split(key, 8)
        s = 0.02
        return {'hidden_states': jax.random.normal(ks[0], (2, 256, D), dtype=jnp.float32), 'Wr': jax.random.normal(ks[1], (D, E), dtype=jnp.float32) * s, 'sWg': jax.random.normal(ks[2], (NS, D, F), dtype=jnp.float32) * s, 'sWu': jax.random.normal(ks[3], (NS, D, F), dtype=jnp.float32) * s, 'sWd': jax.random.normal(ks[4], (NS, F, D), dtype=jnp.float32) * s, 'Wg': jax.random.normal(ks[5], (E, D, F), dtype=jnp.float32) * s, 'Wu': jax.random.normal(ks[6], (E, D, F), dtype=jnp.float32) * s, 'Wd': jax.random.normal(ks[7], (E, F, D), dtype=jnp.float32) * s}
    _L0_ffn_all = _L0_ffn_setup()
    _L0_ffn_in = {k: v for k, v in _L0_ffn_all.items() if k in ('Wr', 'sWg', 'sWu', 'sWd', 'Wg', 'Wu', 'Wd')}
    del _L0_ffn_all
    return {'x': x, 'L0_tok_W_patch': _L0_tok_in['W_patch'], 'L0_tok_b_patch': _L0_tok_in['b_patch'], 'L0_tok_pos_embed': _L0_tok_in['pos_embed'], 'L0_tok_W_coord': _L0_tok_in['W_coord'], 'L0_tok_b_coord': _L0_tok_in['b_coord'], 'L0_tok_W_spinor': _L0_tok_in['W_spinor'], 'L0_tok_b_spinor': _L0_tok_in['b_spinor'], 'L0_tok_W_embed': _L0_tok_in['W_embed'], 'L0_tok_b_embed': _L0_tok_in['b_embed'], 'L0_tok_ln_gamma': _L0_tok_in['ln_gamma'], 'L0_tok_ln_beta': _L0_tok_in['ln_beta'], 'L0_tok_W_out': _L0_tok_in['W_out'], 'L0_tok_b_out': _L0_tok_in['b_out'], 'L0_attn_Wq': _L0_attn_in['Wq'], 'L0_attn_bq': _L0_attn_in['bq'], 'L0_attn_Wk': _L0_attn_in['Wk'], 'L0_attn_bk': _L0_attn_in['bk'], 'L0_attn_Wv': _L0_attn_in['Wv'], 'L0_attn_bv': _L0_attn_in['bv'], 'L0_attn_gn_w': _L0_attn_in['gn_w'], 'L0_attn_gn_b': _L0_attn_in['gn_b'], 'L0_attn_gamma': _L0_attn_in['gamma'], 'L0_ffn_Wr': _L0_ffn_in['Wr'], 'L0_ffn_sWg': _L0_ffn_in['sWg'], 'L0_ffn_sWu': _L0_ffn_in['sWu'], 'L0_ffn_sWd': _L0_ffn_in['sWd'], 'L0_ffn_Wg': _L0_ffn_in['Wg'], 'L0_ffn_Wu': _L0_ffn_in['Wu'], 'L0_ffn_Wd': _L0_ffn_in['Wd']}

def reference(x, L0_tok_W_patch, L0_tok_b_patch, L0_tok_pos_embed, L0_tok_W_coord, L0_tok_b_coord, L0_tok_W_spinor, L0_tok_b_spinor, L0_tok_W_embed, L0_tok_b_embed, L0_tok_ln_gamma, L0_tok_ln_beta, L0_tok_W_out, L0_tok_b_out, L0_attn_Wq, L0_attn_bq, L0_attn_Wk, L0_attn_bk, L0_attn_Wv, L0_attn_bv, L0_attn_gn_w, L0_attn_gn_b, L0_attn_gamma, L0_ffn_Wr, L0_ffn_sWg, L0_ffn_sWu, L0_ffn_sWd, L0_ffn_Wg, L0_ffn_Wu, L0_ffn_Wd):
    import jax
    import jax.numpy as jnp

    def _L0_tok_ref(images, W_patch, b_patch, pos_embed, W_coord, b_coord, W_spinor, b_spinor, W_embed, b_embed, ln_gamma, ln_beta, W_out, b_out):
        import jax, jax.numpy as jnp
        import numpy as np
        IMG = 112
        P = 16
        C = 3
        D = 128
        DC = 8
        DS = 4
        NH = IMG // P
        NPATCH = NH * NH
        PDIM = C * P * P
        BATCH = 32
        EPS = 1e-05
        B = images.shape[0]
        patches = images.reshape(B, C, NH, P, NH, P)
        patches = patches.transpose(0, 2, 4, 1, 3, 5).reshape(B, NPATCH, PDIM)
        x = patches @ W_patch + b_patch + pos_embed
        coords = x @ W_coord + b_coord
        spinor = x @ W_spinor + b_spinor
        K0 = jnp.sum(spinor * spinor, axis=-1)
        x_manifold = coords @ W_embed + b_embed
        x_enh = x_manifold * K0[..., None] + x
        mu = jnp.mean(x_enh, axis=-1, keepdims=True)
        var = jnp.mean(jnp.square(x_enh - mu), axis=-1, keepdims=True)
        x_norm = (x_enh - mu) * jax.lax.rsqrt(var + EPS) * ln_gamma + ln_beta
        return x_norm @ W_out + b_out

    def _L0_attn_ref(x, Wq, bq, Wk, bk, Wv, bv, gn_w, gn_b, gamma):
        import jax, jax.numpy as jnp
        import numpy as np
        B, T, D, H = (2, 512, 128, 8)
        HD = D // H
        EPS = 1e-05
        Bx, Tx, Dx = x.shape

        def proj(W, b):
            return (x @ W.T + b).reshape(Bx, Tx, H, HD).transpose(0, 2, 1, 3)
        Q, K, V = (proj(Wq, bq), proj(Wk, bk), proj(Wv, bv))
        attn = jnp.einsum('bhqd,bhkd->bhqk', Q, K)
        idx = jnp.arange(Tx)
        diff = idx[:, None] - idx[None, :]
        decay = jnp.where(diff >= 0, jnp.power(gamma, jnp.maximum(diff, 0).astype(jnp.float32)), 0.0)
        attn = attn * decay[None, None]
        out = jnp.einsum('bhqk,bhkd->bhqd', attn, V)
        out = out.transpose(0, 2, 1, 3)
        mean = out.mean(axis=(1, 3), keepdims=True)
        var = out.var(axis=(1, 3), keepdims=True)
        out = (out - mean) / jnp.sqrt(var + EPS)
        out = out.reshape(Bx, Tx, Dx) * gn_w + gn_b
        return out

    def _L0_ffn_ref(hidden_states, Wr, sWg, sWu, sWd, Wg, Wu, Wd):
        import jax, jax.numpy as jnp
        import numpy as np
        E = 64
        K = 6
        NS = 2
        D = 128
        F = 128

        def _swiglu_ffn(x, wg, wu, wd):
            return jax.nn.silu(x @ wg) * (x @ wu) @ wd
        B, S, d = hidden_states.shape
        x = hidden_states.reshape(-1, d)
        N = x.shape[0]
        shared = jnp.zeros_like(x)
        for e in range(NS):
            shared = shared + _swiglu_ffn(x, sWg[e], sWu[e], sWd[e])
        logits = x @ Wr
        probs = jax.nn.softmax(logits, axis=-1)
        top_w, top_i = jax.lax.top_k(probs, K)
        top_w = top_w / jnp.sum(top_w, axis=-1, keepdims=True)
        gate = jnp.zeros((N, E), dtype=x.dtype).at[jnp.arange(N)[:, None], top_i].set(top_w)
        routed = jnp.zeros_like(x)
        for e in range(E):
            routed = routed + _swiglu_ffn(x, Wg[e], Wu[e], Wd[e]) * gate[:, e:e + 1]
        out = (shared + routed + x).reshape(B, S, d)
        return out
    h = _L0_tok_ref(x, L0_tok_W_patch, L0_tok_b_patch, L0_tok_pos_embed, L0_tok_W_coord, L0_tok_b_coord, L0_tok_W_spinor, L0_tok_b_spinor, L0_tok_W_embed, L0_tok_b_embed, L0_tok_ln_gamma, L0_tok_ln_beta, L0_tok_W_out, L0_tok_b_out)
    h = h + _L0_attn_ref(_layernorm(h, axis=-1), L0_attn_Wq, L0_attn_bq, L0_attn_Wk, L0_attn_bk, L0_attn_Wv, L0_attn_bv, L0_attn_gn_w, L0_attn_gn_b, L0_attn_gamma)
    h = h + _L0_ffn_ref(_layernorm(h, axis=-1), L0_ffn_Wr, L0_ffn_sWg, L0_ffn_sWu, L0_ffn_sWd, L0_ffn_Wg, L0_ffn_Wu, L0_ffn_Wd)
    return h

_drawn_inputs = setup_inputs


def setup_inputs(seed=0):
    import zlib

    import numpy as np

    out = dict(_drawn_inputs(seed))
    spreads = {'L0_tok_b_patch': (0.0, 0.1),
     'L0_tok_b_coord': (0.0, 0.1),
     'L0_tok_b_spinor': (0.0, 0.1),
     'L0_tok_b_embed': (0.0, 0.1),
     'L0_tok_ln_gamma': (1.0, 0.2),
     'L0_tok_ln_beta': (0.0, 0.1),
     'L0_tok_b_out': (0.0, 0.1),
     'L0_attn_bq': (0.0, 0.1),
     'L0_attn_bk': (0.0, 0.1),
     'L0_attn_bv': (0.0, 0.1),
     'L0_attn_gn_w': (1.0, 0.2),
     'L0_attn_gn_b': (0.0, 0.1)}
    factors = {'L0_ffn_Wr': 8.0,
     'L0_ffn_sWg': 8.0,
     'L0_ffn_sWu': 8.0,
     'L0_ffn_sWd': 8.0,
     'L0_ffn_Wg': 8.0,
     'L0_ffn_Wu': 8.0,
     'L0_ffn_Wd': 8.0}
    for name, (base, spread) in spreads.items():
        noise = np.random.default_rng([zlib.crc32(name.encode()), seed]).standard_normal(out[name].shape)
        drawn = base * np.exp(spread * noise) if base else spread * noise
        out[name] = jnp.asarray(drawn.astype(out[name].dtype))
    for name, factor in factors.items():
        out[name] = (out[name] * factor).astype(out[name].dtype)
    return out
```

```python
from contextlib import ExitStack

import numpy as np

import concourse.bass as bass
from concourse import mybir

ALU = mybir.AluOpType
ACT = mybir.ActivationFunctionType
AX = mybir.AxisListType
F32 = mybir.dt.float32
F32R = mybir.dt.float32r

BATCH, CHANNELS, IMG, PATCH = 16, 3, 112, 16
GRID = IMG // PATCH
SEQ = GRID * GRID
TOKENS = BATCH * SEQ
DIM = 128
PDIM = CHANNELS * PATCH * PATCH
KCHUNKS = PDIM // 128
COORD, SPINOR = 8, 4
CS = COORD + SPINOR
HEADS = 8
HD = DIM // HEADS
EXPERTS, SHARED, TOPK = 64, 2, 6
ALL_EXPERTS = EXPERTS + SHARED
EPS = 1e-5

PAIR = 2 * SEQ
PAIRS = TOKENS // PAIR
HALF = TOKENS // 2
QUAD = PAIRS // 2
BITS = 6
SENT = 8
WCOLS = 3 * DIM
STEP = 3
ROUNDS = ALL_EXPERTS // STEP
UNITS = 2 * STEP
RING = 3
LAG = 2
WLOADS = 6


def layout_constants():
    c128 = np.zeros((128, 128 + 128 + HEADS + 1), np.float32)
    c128[:, 0:128] = np.eye(128)
    c128[:, 128:256] = np.eye(128) - 1.0 / 128
    c128[:, 256:256 + HEADS] = np.arange(128)[:, None] // HD == np.arange(HEADS)[None, :]
    c128[:, 256 + HEADS] = 1.0 / 128
    tok = np.arange(PAIR)
    same = tok[:, None] // SEQ == tok[None, :] // SEQ
    diff = tok[None, :] - tok[:, None]
    keep = same & (diff >= 0)
    cpair = np.zeros((PAIR, PAIR + 2 * BITS * PAIR), np.float32)
    cpair[:, 0:PAIR] = same
    for b in range(BITS):
        bit = (np.maximum(diff, 0) >> b) & 1
        mask = keep if b == 0 else np.ones_like(keep)
        cpair[:, PAIR * (1 + b):PAIR * (2 + b)] = bit * mask
        cpair[:, PAIR * (1 + BITS + b):PAIR * (2 + BITS + b)] = (1 - bit) * mask
    return c128, cpair


def build(nc, patches, w_patch, pos, cols, bias_cs, rows, small_w, embed_w, gamma, c128_d, cpair_d,
          experts_w, out):
    with ExitStack() as ctx:
        def sb(name, shape, dt=F32):
            return ctx.enter_context(nc.sbuf_tensor(name, shape, dt))

        def sem(name):
            return ctx.enter_context(nc.semaphore(name))

        gates_dram = nc.dram_tensor("gates_dram", [ALL_EXPERTS, TOKENS], F32, kind="Internal").ap()

        raw_w = sb("raw_w", [128, ALL_EXPERTS, WCOLS])
        c128 = sb("c128", [128, 256 + HEADS + 1])
        cpair = sb("cpair", [PAIR, PAIR * (1 + 2 * BITS)])
        colv = sb("colv", [128, 6])
        csb = sb("csb", [CS, 1])
        rowv = sb("rowv", [PAIR, 4, DIM])
        smallw = sb("smallw", [128, CS + 4 * DIM + EXPERTS])
        embw = sb("embw", [CS, 2 * DIM])
        posT = sb("posT", [128, SEQ])
        gam = sb("gam", [PAIR, BITS])
        ident = c128[:, 0:128]
        center = c128[:, 128:256]
        head_mask = c128[:, 256:256 + HEADS]
        mean_col = c128[:, 256 + HEADS:257 + HEADS]
        same_image = cpair[:, 0:PAIR]
        b_patch, b_embed, ln_gamma, ln_beta, bq, bk = (colv[:, i:i + 1] for i in range(6))
        b_out, bv, gn_w, gn_b = (rowv[:, i, :] for i in range(4))
        w_cs = smallw[:, 0:CS]
        w_out, w_q, w_k, w_v = (smallw[:, CS + i * DIM:CS + (i + 1) * DIM] for i in range(4))
        w_router = smallw[:, CS + 4 * DIM:]

        big = sb("big", [128, 8 * TOKENS])
        pat = big[:, 0:KCHUNKS * TOKENS].rearrange("p (k t) -> p k t", k=KCHUNKS)
        wpat = big[:, KCHUNKS * TOKENS:KCHUNKS * TOKENS + PDIM].rearrange("p (k n) -> p k n", k=KCHUNKS)
        q_blk = big[:, :].rearrange("p (h t) -> p h t", h=HEADS)
        silu, gated_up, hid = (big[:, i * RING * HALF:(i + 1) * RING * HALF].rearrange("p (r n) -> p r n", r=RING)
                               for i in range(3))

        tA = sb("tA", [128, TOKENS])
        tB = sb("tB", [128, TOKENS])
        tC = sb("tC", [128, TOKENS])
        w_og = sb("w_og", [128, DIM])
        beta_bc = sb("beta_bc", [128, PAIR])
        bq_mask = sb("bq_mask", [128, HEADS])
        h_tok = sb("h_tok", [PAIR, PAIRS, DIM])
        n_tok = sb("n_tok", [PAIR, PAIRS, DIM])
        v_tok = sb("v_tok", [PAIR, PAIRS, DIM])
        out_bias = sb("out_bias", [PAIR, DIM])
        decay = sb("decay", [PAIR, PAIR])
        dfac = sb("dfac", [PAIR, PAIR])
        attn = sb("attn", [PAIR, 2, HEADS * PAIR])
        cs_val, cs_sq = attn[0:CS, 0, :], attn[0:CS, 1, :]
        gateT = attn[0:EXPERTS, 0, :]
        stat = sb("stat", [PAIR, PAIRS, 6])
        mv = sb("mv", [PAIR, PAIRS, 2])
        r0 = sb("r0", [PAIR, PAIRS])
        rstd = sb("rstd", [PAIR, PAIRS])
        half_neg = sb("half_neg", [PAIR, HEADS * PAIRS])
        g_sum = sb("g_sum", [PAIR, HEADS * PAIRS])
        g_mean = sb("g_mean", [PAIR, HEADS * PAIRS])
        g_rstd = sb("g_rstd", [PAIR, HEADS * PAIRS])
        prob = sb("prob", [PAIR, PAIRS, EXPERTS + SENT])
        gate = sb("gate", [PAIR, PAIRS, EXPERTS])
        repl = v_tok[:, :, :].rearrange("p c n -> p (c n)")[:, 0:PAIRS * (EXPERTS + SENT)].rearrange(
            "p (c n) -> p c n", c=PAIRS)
        top8 = sb("top8", [PAIR, PAIRS, 8])
        r_stat = sb("r_stat", [PAIR, 4, PAIRS])
        ones_row = sb("ones_row", [SHARED, TOKENS])
        x_hi = sb("x_hi", [128, TOKENS], F32R)
        x_lo = sb("x_lo", [128, TOKENS], F32R)
        w_hi = sb("w_hi", [128, STEP, WCOLS], F32R)
        w_lo = sb("w_lo", [128, STEP, WCOLS], F32R)
        gate_bc = sb("gate_bc", [128, STEP, TOKENS])
        hid_hi = sb("hid_hi", [128, RING, HALF], F32R)
        hid_lo = sb("hid_lo", [128, RING, HALF], F32R)

        ps = ctx.enter_context(nc.psum_tensor("ps", [128, 8, 512], F32))

        def half(bank, j, m=128):
            return ps[0:m, bank + j, 0:HALF]

        def both(bank, m=128):
            return ps[0:m, bank:bank + 2, 0:HALF]

        def chunk(bank, c, m=PAIR):
            return ps[0:m, bank + c // QUAD, (c % QUAD) * DIM:(c % QUAD + 1) * DIM]

        def chunks(bank, j):
            return ps[0:PAIR, bank + j, :].rearrange("p (c n) -> p c n", n=DIM)

        def turned(bank, c, m=128):
            return ps[0:m, bank + c // QUAD, (c % QUAD) * PAIR:(c % QUAD + 1) * PAIR]

        def cols2(t):
            return t[:, :].rearrange("p (j n) -> p j n", j=2)

        def hs(j):
            return slice(j * HALF, (j + 1) * HALF)

        def pr(c):
            return slice(c * PAIR, (c + 1) * PAIR)

        def over_dim(t):
            return t.unsqueeze(2).broadcast_to([PAIR, PAIRS, DIM])

        in_w = sem("in_w")
        in_patch = [sem(f"in_patch{k}") for k in range(KCHUNKS)]
        in_small = sem("in_small")
        in_const = sem("in_const")
        in_experts = sem("in_experts")
        ones_stored = sem("ones_stored")
        gates_stored = sem("gates_stored")
        gate_in = [sem(f"gate_in{k}") for k in range(STEP)]
        out_stored = sem("out_stored")
        p_embed = sem("p_embed")
        p_cs = sem("p_cs")
        p_man = sem("p_man")
        p_center = sem("p_center")
        p_bias = sem("p_bias")
        p_h = sem("p_h")
        p_turn1 = sem("p_turn1")
        p_q = sem("p_q")
        p_k = sem("p_k")
        p_v = sem("p_v")
        p_score = sem("p_score")
        p_attn = sem("p_attn")
        p_gmean = sem("p_gmean")
        p_gvar = sem("p_gvar")
        p_turn2 = sem("p_turn2")
        p_logit = sem("p_logit")
        p_resT = sem("p_resT")
        p_gateT = sem("p_gateT")
        a_cs = sem("a_cs")
        a_man = sem("a_man")
        a_sq = sem("a_sq")
        a_turn1 = sem("a_turn1")
        a_q = sem("a_q")
        a_k = sem("a_k")
        a_gmean = sem("a_gmean")
        a_gsq = sem("a_gsq")
        a_xhi = sem("a_xhi")
        a_exp = sem("a_exp")
        a_resT = sem("a_resT")
        g_prep = sem("g_prep")
        g_decay = sem("g_decay")
        g_pow = sem("g_pow")
        g_res = sem("g_res")
        v_prep = sem("v_prep")
        v_x = sem("v_x")
        v_enh = sem("v_enh")
        v_xc = sem("v_xc")
        v_bias = sem("v_bias")
        v_var = sem("v_var")
        v_norm = sem("v_norm")
        v_turn1 = sem("v_turn1")
        v_v = sem("v_v")
        v_mask = sem("v_mask")
        v_gsum = sem("v_gsum")
        v_cen = sem("v_cen")
        v_h2 = sem("v_h2")
        v_y2T = sem("v_y2T")
        v_xlo = sem("v_xlo")
        v_logit = sem("v_logit")
        v_gate = sem("v_gate")
        v_gateT = sem("v_gateT")
        dve_chain = sem("dve_chain")
        pool_chain = sem("pool_chain")
        w_hi_ready = sem("w_hi_ready")
        w_lo_ready = sem("w_lo_ready")
        gate_ready = sem("gate_ready")
        up_ready = sem("up_ready")
        silu_ready = sem("silu_ready")
        gated_ready = sem("gated_ready")
        hid_ready = sem("hid_ready")
        hid_hi_ready = sem("hid_hi_ready")
        hid_lo_ready = sem("hid_lo_ready")
        down_done = sem("down_done")
        fin_ready = sem("fin_ready")

        block = ctx.enter_context(nc.Block())

        def at_least(eng, s, value):
            if isinstance(value, int) and value <= 0:
                return
            eng.wait_ge(s, value)

        @block.sync
        def _(sp):
            sp.dma_start(wpat, w_patch).then_inc(in_w, 16)
            for k in range(KCHUNKS):
                sp.dma_start(pat[:, k, :], patches[:, k, :]).then_inc(in_patch[k], 16)
                if k == 0:
                    sp.dma_start(colv[:], cols).then_inc(in_small, 16)
                    sp.dma_start(posT[:], pos).then_inc(in_small, 16)
                    sp.dma_start(csb[:], bias_cs).then_inc(in_small, 16)
                    sp.dma_start(smallw[:], small_w).then_inc(in_small, 16)
                    sp.dma_start(embw[:], embed_w).then_inc(in_small, 16)
            sp.dma_start(c128[:], c128_d).then_inc(in_const, 16)
            sp.dma_start(rowv[:], rows.broadcast_to([PAIR, 4, DIM])).then_inc(in_const, 16)
            sp.dma_start(gam[:, 0:1], gamma.broadcast_to([PAIR, 1])).then_inc(in_const, 16)
            sp.dma_start(cpair[:], cpair_d).then_inc(in_const, 16)
            n = ALL_EXPERTS // WLOADS
            for g in range(WLOADS):
                sp.dma_start(raw_w[:, g * n:(g + 1) * n, :], experts_w[:, g * n:(g + 1) * n, :]).then_inc(in_experts, 16)
            sp.wait_ge(g_prep, 1)
            sp.dma_start(gates_dram[0:SHARED, :], ones_row[:]).then_inc(ones_stored, 16)
            sp.wait_ge(ones_stored, 16)

            def load_gate(e, k):
                sp.dma_start(gate_bc[:, k, :], gates_dram[bass.ds(e, 1), :].broadcast_to([128, TOKENS])).then_inc(gate_in[k], 16)

            for e in range(SHARED):
                load_gate(e, e)
            sp.wait_ge(v_gateT, 1)
            sp.dma_start(gates_dram[SHARED:, :], gateT).then_inc(gates_stored, 16)
            sp.wait_ge(gates_stored, 16)
            for e in range(SHARED, STEP):
                load_gate(e, e)
            with sp.Fori(1, ROUNDS) as t:
                for k in range(STEP):
                    sp.wait_ge(gated_ready, UNITS * t - UNITS + 2 * k + 2)
                    load_gate(STEP * t + k, k)
            for j in range(2):
                sp.wait_ge(fin_ready, j + 1)
                sp.dma_start(out[:, hs(j)], tC[:, hs(j)]).then_inc(out_stored, 16)
            sp.wait_ge(out_stored, 32)

        @block.gpsimd
        def _(pool):
            steps = [0]

            def link(ins):
                steps[0] += 1
                ins.then_inc(pool_chain, 1)
                pool.wait_ge(pool_chain, steps[0])

            nc.gpsimd.memset(ones_row[:], 1.0).then_inc(g_prep, 1)
            nc.gpsimd.memset(half_neg[:], -0.5).then_inc(g_prep, 1)
            nc.gpsimd.memset(prob[:, :, EXPERTS:], -1.0).then_inc(g_prep, 1)
            pool.wait_ge(in_const, 64)
            for b in range(1, BITS):
                link(nc.gpsimd.tensor_tensor(gam[:, b:b + 1], gam[:, b - 1:b], gam[:, b - 1:b], ALU.mult))
            for b in range(BITS):
                bit = cpair[:, PAIR * (1 + b):PAIR * (2 + b)]
                nbit = cpair[:, PAIR * (1 + BITS + b):PAIR * (2 + BITS + b)]
                dst = decay[:] if b == 0 else dfac[:]
                link(nc.gpsimd.tensor_scalar(dst, bit, gam[:, b:b + 1], None, ALU.mult))
                link(nc.gpsimd.tensor_tensor(dst, dst, nbit, ALU.add))
                if b:
                    link(nc.gpsimd.tensor_tensor(decay[:], decay[:], dfac[:], ALU.mult))
            pool.wait_ge(g_prep, 3)

            def inverse_root(n, out_ap, in_ap, width):
                pool.wait_ge(v_var, n)
                nc.gpsimd.tensor_tensor(out_ap, in_ap, half_neg[:, 0:width], ALU.pow).then_inc(g_pow, 1)

            for n in range(2):
                inverse_root(n + 1, rstd[:], r0[:], PAIRS)
            pool.wait_ge(v_norm, 1)
            nc.gpsimd.tensor_tensor(h_tok[:], h_tok[:], gn_b.unsqueeze(1).broadcast_to([PAIR, PAIRS, DIM]),
                                    ALU.add).then_inc(g_res, 1)
            inverse_root(3, g_rstd[:], g_sum[:], HEADS * PAIRS)
            inverse_root(4, rstd[:], r0[:], PAIRS)
            pool.wait_ge(v_norm, 2)
            nc.gpsimd.tensor_tensor(h_tok[:], h_tok[:], n_tok[:], ALU.add).then_inc(g_res, 1)

        @block.scalar
        def _(act):
            def copy(out_ap, in_ap, s):
                nc.scalar.activation(out_ap, in_ap, ACT.Copy).then_inc(s, 1)

            act.wait_ge(in_small, 80)
            for j in range(2):
                act.wait_ge(p_cs, j + 1)
                nc.scalar.activation(cs_val[:, hs(j)], half(2, j, CS), ACT.Identity, bias=csb[:, 0:1]).then_inc(a_cs, 1)
                nc.scalar.activation(cs_sq[:, hs(j)], half(2, j, CS), ACT.Square, bias=csb[:, 0:1]).then_inc(a_cs, 1)
            for j in range(2):
                act.wait_ge(p_man, 2 * j + 1)
                nc.scalar.activation(tB[:, hs(j)], half(4, j), ACT.Identity, bias=b_embed).then_inc(a_man, 1)
            for j in range(2):
                act.wait_ge(p_center, j + 1)
                if j == 0:
                    act.wait_ge(v_enh, 2)
                nc.scalar.activation(tB[:, hs(j)], half(0, j), ACT.Square).then_inc(a_sq, 1)
            act.wait_ge(in_const, 64)
            nc.scalar.activation(bq_mask[:], head_mask, ACT.Copy, scale=bq).then_inc(a_q, 1)
            act.wait_ge(p_turn1, 1)
            copy(tA[:, hs(0)], half(6, 0), a_turn1)
            act.wait_ge(a_q, 1)
            act.wait_ge(p_q, 1)
            for h in range(HEADS // 2):
                nc.scalar.activation(q_blk[:, h, hs(0)], half(0, 0), ACT.Identity, bias=bq_mask[:, h:h + 1],
                                     scale=head_mask[:, h:h + 1]).then_inc(a_q, 1)
            act.wait_ge(p_k, 1)
            nc.scalar.activation(tB[:, hs(0)], half(2, 0), ACT.Identity, bias=bk).then_inc(a_k, 1)
            act.wait_ge(p_q, 2)
            for h in range(HEADS // 2):
                nc.scalar.activation(q_blk[:, h, hs(1)], half(0, 1), ACT.Identity, bias=bq_mask[:, h:h + 1],
                                     scale=head_mask[:, h:h + 1]).then_inc(a_q, 1)
            act.wait_ge(p_k, 2)
            nc.scalar.activation(tB[:, hs(1)], half(2, 1), ACT.Identity, bias=bk).then_inc(a_k, 1)
            act.wait_ge(p_gmean, 1)
            nc.scalar.activation(g_mean[:], ps[0:PAIR, 6, 0:HEADS * PAIRS], ACT.Copy,
                                 scale=1.0 / (SEQ * HD)).then_inc(a_gmean, 1)
            for j in range(2):
                act.wait_ge(v_cen, j + 1)
                nc.scalar.activation(v_tok[:, j * QUAD:(j + 1) * QUAD, :], n_tok[:, j * QUAD:(j + 1) * QUAD, :],
                                     ACT.Square).then_inc(a_gsq, 1)
            for j in range(2):
                act.wait_ge(p_turn2, j + 1)
                copy(x_hi[:, hs(j)], half(6, j), a_xhi)
            act.wait_ge(in_experts, 16 * WLOADS)

            def weight_hi(e, k):
                at_least(act, down_done, 2 * e - 2 * STEP + 2)
                nc.scalar.activation(w_hi[:, k, :], raw_w[:, e, :] if isinstance(e, int) else
                                     raw_w[:, bass.ds(e, 1), :].rearrange("p o n -> p (o n)"),
                                     ACT.Copy).then_inc(w_hi_ready, 1)

            weight_hi(0, 0)
            act.wait_ge(v_logit, 1)
            nc.scalar.activation(prob[:, :, 0:EXPERTS], gate[:], ACT.Exp).then_inc(a_exp, 1)
            act.wait_ge(p_resT, 1)
            nc.scalar.activation(cols2(tA), both(2), ACT.Copy).then_inc(a_resT, 1)

            def hidden_hi(n, k):
                act.wait_ge(hid_ready, n + 1)
                at_least(act, down_done, n - RING + 1)
                nc.scalar.activation(hid_hi[:, k, :], hid[:, k, :], ACT.Copy).then_inc(hid_hi_ready, 1)

            def rounds(t, first):
                for u in range(UNITS):
                    n = UNITS * t + u
                    act.wait_ge(gate_ready, n + 1)
                    at_least(act, hid_ready, n - RING + 1)
                    nc.scalar.activation(silu[:, u % RING, :], ps[:, 2 * (u % RING), 0:HALF], ACT.Silu).then_inc(silu_ready, 1)
                    if not (first and u == 0):
                        hidden_hi(n - 1, (u - 1) % RING)
                    if u % 2:
                        k = (u // 2 + 1) % STEP
                        if isinstance(t, int) or u < UNITS - 1:
                            weight_hi(STEP * t + u // 2 + 1, k)
                        else:
                            weight_hi(nxt(t), k)

            def nxt(t):
                return STEP * t + STEP

            rounds(0, True)
            with act.Fori(1, ROUNDS - 1) as t:
                rounds(t, False)
            last = ROUNDS - 1
            for u in range(UNITS):
                n = UNITS * last + u
                act.wait_ge(gate_ready, n + 1)
                act.wait_ge(hid_ready, n - RING + 1)
                nc.scalar.activation(silu[:, u % RING, :], ps[:, 2 * (u % RING), 0:HALF], ACT.Silu).then_inc(silu_ready, 1)
                hidden_hi(n - 1, (u - 1) % RING)
                if u % 2 and u < UNITS - 1:
                    weight_hi(STEP * last + u // 2 + 1, u // 2 + 1)
            hidden_hi(UNITS * ROUNDS - 1, (UNITS - 1) % RING)

        @block.vector
        def _(dve):
            steps = [0]

            def link(ins):
                steps[0] += 1
                ins.then_inc(dve_chain, 1)
                dve.wait_ge(dve_chain, steps[0])

            dve.wait_ge(in_small, 80)
            nc.vector.tensor_scalar(w_og[:], w_out, ln_gamma, None, ALU.mult).then_inc(v_prep, 1)
            nc.vector.tensor_copy(beta_bc[:], ln_beta.broadcast_to([128, PAIR])).then_inc(v_prep, 1)
            for j in range(2):
                dve.wait_ge(p_embed, j + 1)
                nc.vector.scalar_tensor_tensor(
                    out=tA[:, hs(j)].rearrange("p (b s) -> p b s", s=SEQ),
                    in0=half(0, j).rearrange("p (b s) -> p b s", s=SEQ), scalar=b_patch,
                    in1=posT[:].unsqueeze(1).broadcast_to([128, BATCH // 2, SEQ]),
                    op0=ALU.add, op1=ALU.add).then_inc(v_x, 1)
            for j in range(2):
                dve.wait_ge(a_man, j + 1)
                dve.wait_ge(p_man, 2 * j + 2)
                link(nc.vector.tensor_tensor(tC[:, hs(j)], half(6, j), tB[:, hs(j)], ALU.mult))
                nc.vector.tensor_tensor(tC[:, hs(j)], tC[:, hs(j)], tA[:, hs(j)], ALU.add).then_inc(v_enh, 1)
            for j in range(2):
                dve.wait_ge(p_center, j + 1)
                if j == 0:
                    dve.wait_ge(a_sq, 1)
                else:
                    dve.wait_ge(a_sq, 2)
                nc.vector.tensor_copy(tA[:, hs(j)], half(0, j)).then_inc(v_xc, 1)
            dve.wait_ge(in_const, 64)
            dve.wait_ge(p_bias, 1)
            nc.vector.tensor_tensor(out_bias[:], ps[0:PAIR, 5, 0:DIM], b_out, ALU.add).then_inc(v_bias, 1)
            dve.wait_ge(p_h, PAIRS)
            nc.vector.tensor_scalar(r0[:], ps[0:PAIR, 4, 0:PAIRS], EPS, None, ALU.add).then_inc(v_var, 1)
            dve.wait_ge(g_pow, 1)
            dve.wait_ge(v_bias, 1)

            def row_stats(n, make):
                for c in range(PAIRS):
                    if make:
                        make(c)
                for c in range(PAIRS):
                    last = nc.vector.bn_stats(stat[:, c, :], h_tok[:, c, :])
                link(last)
                for c in range(PAIRS):
                    last = nc.vector.bn_aggr(mv[:, c, :], stat[:, c, :])
                link(last)
                nc.vector.tensor_scalar(r0[:], mv[:, :, 1], EPS, None, ALU.add).then_inc(v_var, 1)

            def row_norm(s):
                for c in range(PAIRS):
                    last = nc.vector.tensor_scalar(n_tok[:, c, :], h_tok[:, c, :], mv[:, c, 0:1], rstd[:, c:c + 1],
                                                   ALU.subtract, ALU.mult)
                last.then_inc(s, 1)

            def make_h(c):
                ins = nc.vector.scalar_tensor_tensor(out=h_tok[:, c, :], in0=chunk(2, c), scalar=rstd[:, c:c + 1],
                                                     in1=out_bias[:], op0=ALU.mult, op1=ALU.add)
                if c == PAIRS - 1:
                    link(ins)

            row_stats(2, make_h)
            dve.wait_ge(g_pow, 2)
            row_norm(v_norm)
            dve.wait_ge(p_turn1, 2)
            nc.vector.tensor_copy(tA[:, hs(1)], half(6, 1)).then_inc(v_turn1, 1)
            dve.wait_ge(a_q, 1)
            for j in range(2):
                dve.wait_ge(p_q, j + 1)
                dve.wait_ge(a_q, 1 + HEADS // 2 * (j + 1))
                for h in range(HEADS // 2, HEADS):
                    ins = nc.vector.tensor_scalar(q_blk[:, h, hs(j)], half(0, j), head_mask[:, h:h + 1],
                                                  bq_mask[:, h:h + 1], ALU.mult, ALU.add)
                ins.then_inc(v_prep, 1)
            for j in range(2):
                dve.wait_ge(p_v, j + 1)
                nc.vector.tensor_tensor(v_tok[:, j * QUAD:(j + 1) * QUAD, :], chunks(4, j),
                                        bv.unsqueeze(1).broadcast_to([PAIR, QUAD, DIM]), ALU.add).then_inc(v_v, 1)
            dve.wait_ge(pool_chain, POOL_DECAY)
            for c in range(PAIRS):
                for g in range(2):
                    dve.wait_ge(p_score, 2 * c + g + 1)
                    if c >= 2:
                        dve.wait_ge(p_attn, c - 1)
                    bank = SCORE_BANKS[c % 3] + g
                    w = HEADS // 2
                    nc.vector.tensor_tensor(
                        attn[:, c % 2, g * HALF:(g + 1) * HALF].rearrange("p (h q) -> p h q", h=w),
                        ps[0:PAIR, bank, 0:HALF].rearrange("p (h q) -> p h q", h=w),
                        decay[:].unsqueeze(1).broadcast_to([PAIR, w, PAIR]), ALU.mult).then_inc(v_mask, 1)
            groups = HEADS * PAIRS

            def by_head(ap):
                return ap.rearrange("p c (h d) -> p (c h) d", d=HD)

            attn_out = ps[0:PAIR, 2:4, :].rearrange("p b (g d) -> p (b g) d", d=HD)
            dve.wait_ge(p_attn, PAIRS)
            nc.vector.tensor_reduce(g_sum[:], attn_out, AX.X, ALU.add).then_inc(v_gsum, 1)
            dve.wait_ge(a_gmean, 1)
            gh = groups // 2
            for j in range(2):
                nc.vector.tensor_tensor(by_head(n_tok[:, j * QUAD:(j + 1) * QUAD, :]), attn_out[:, j * gh:(j + 1) * gh, :],
                                        g_mean[:, j * gh:(j + 1) * gh].unsqueeze(2).broadcast_to([PAIR, gh, HD]),
                                        ALU.subtract).then_inc(v_cen, 1)
            for j in range(2):
                dve.wait_ge(a_gsq, j + 1)
                nc.vector.tensor_reduce(g_sum[:, j * gh:(j + 1) * gh], by_head(v_tok[:, j * QUAD:(j + 1) * QUAD, :]),
                                        AX.X, ALU.add).then_inc(v_gsum, 1)
            dve.wait_ge(p_gvar, 1)
            nc.vector.tensor_scalar(g_sum[:], ps[0:PAIR, 7, 0:groups], 1.0 / (SEQ * HD), EPS,
                                    ALU.mult, ALU.add).then_inc(v_var, 1)
            dve.wait_ge(g_pow, 3)
            dve.wait_ge(v_cen, 2)
            dve.wait_ge(g_res, 1)
            link(nc.vector.tensor_tensor(by_head(n_tok[:]), by_head(n_tok[:]),
                                         g_rstd[:].unsqueeze(2).broadcast_to([PAIR, groups, HD]), ALU.mult))
            link(nc.vector.tensor_tensor(n_tok[:], n_tok[:], gn_w.unsqueeze(1).broadcast_to([PAIR, PAIRS, DIM]), ALU.mult))
            link(nc.vector.tensor_tensor(h_tok[:], h_tok[:], n_tok[:], ALU.add))
            row_stats(4, None)
            dve.wait_ge(g_pow, 4)
            row_norm(v_norm)
            for j in range(2):
                dve.wait_ge(p_turn2, j + 1)
                dve.wait_ge(a_xhi, j + 1)
                nc.vector.tensor_copy(tB[:, hs(j)], half(6, j)).then_inc(v_y2T, 1)
            for j in range(2):
                nc.vector.tensor_tensor(x_lo[:, hs(j)], half(6, j), x_hi[:, hs(j)].bitcast(F32),
                                        ALU.subtract).then_inc(v_xlo, 1)
            def weight_lo(e, k):
                dve.wait_ge(w_hi_ready, e + 1)
                at_least(dve, down_done, 2 * e - 2 * STEP + 2)
                src = raw_w[:, e, :] if isinstance(e, int) else raw_w[:, bass.ds(e, 1), :].rearrange("p o n -> p (o n)")
                nc.vector.tensor_tensor(w_lo[:, k, :], src, w_hi[:, k, :].bitcast(F32), ALU.subtract).then_inc(w_lo_ready, 1)

            weight_lo(0, 0)
            logits = ps[0:PAIR, 4, :].rearrange("p (c e) -> p c e", e=EXPERTS)
            over_experts = [PAIR, PAIRS, EXPERTS]
            probs = prob[:, :, 0:EXPERTS]
            dve.wait_ge(p_logit, 1)
            link(nc.vector.tensor_reduce(r_stat[:, 0, :], logits, AX.X, ALU.max))
            nc.vector.tensor_tensor(gate[:], logits, r_stat[:, 0, :].unsqueeze(2).broadcast_to(over_experts),
                                    ALU.subtract).then_inc(v_logit, 1)
            dve.wait_ge(a_exp, 1)
            link(nc.vector.tensor_reduce(r_stat[:, 1, :], probs, AX.X, ALU.add))
            link(nc.vector.reciprocal(r_stat[:, 2, :], r_stat[:, 1, :]))
            dve.wait_ge(g_prep, 3)
            link(nc.vector.tensor_tensor(probs, probs, r_stat[:, 2, :].unsqueeze(2).broadcast_to(over_experts), ALU.mult))
            for c in range(PAIRS):
                last = nc.vector.max(top8[:, c, :], prob[:, c, :])
            link(last)
            link(nc.vector.memset(top8[:, :, TOPK:], -1.0))
            for c in range(PAIRS):
                last = nc.vector.match_replace(repl[:, c, :], top8[:, c, :], prob[:, c, :], -2.0)
            link(last)
            link(nc.vector.tensor_reduce(r_stat[:, 0, :], top8[:, :, 0:TOPK], AX.X, ALU.add))
            link(nc.vector.reciprocal(r_stat[:, 3, :], r_stat[:, 0, :]))
            link(nc.vector.scalar_tensor_tensor(out=gate[:], in0=repl[:, :, 0:EXPERTS], scalar=-1.5, in1=probs,
                                                op0=ALU.is_lt, op1=ALU.mult))
            nc.vector.tensor_tensor(gate[:], gate[:], r_stat[:, 3, :].unsqueeze(2).broadcast_to(over_experts),
                                    ALU.mult).then_inc(v_gate, 1)
            dve.wait_ge(p_gateT, 1)
            nc.vector.tensor_copy(cols2(gateT), both(4, EXPERTS)).then_inc(v_gateT, 1)

            def hidden_lo(n, k):
                dve.wait_ge(hid_hi_ready, n + 1)
                at_least(dve, down_done, n - RING + 1)
                nc.vector.tensor_tensor(hid_lo[:, k, :], hid[:, k, :], hid_hi[:, k, :].bitcast(F32),
                                        ALU.subtract).then_inc(hid_lo_ready, 1)

            def rounds(t, first, final):
                for u in range(UNITS):
                    n = UNITS * t + u
                    k = u % RING
                    dve.wait_ge(up_ready, n + 1)
                    dve.wait_ge(gate_in[u // 2], 16 * t + 16)
                    at_least(dve, hid_ready, n - RING + 1)
                    nc.vector.tensor_tensor(gated_up[:, k, :], ps[:, 2 * k + 1, 0:HALF],
                                            gate_bc[:, u // 2, hs(u % 2)], ALU.mult).then_inc(gated_ready, 1)
                    dve.wait_ge(silu_ready, n + 1)
                    dve.wait_ge(gated_ready, n + 1)
                    at_least(dve, hid_lo_ready, n - RING + 1)
                    at_least(dve, hid_hi_ready, n - RING + 1)
                    nc.vector.tensor_tensor(hid[:, k, :], gated_up[:, k, :], silu[:, k, :], ALU.mult).then_inc(hid_ready, 1)
                    if not (first and u == 0):
                        hidden_lo(n - 1, (u - 1) % RING)
                    if u % 2 and not (final and u == UNITS - 1):
                        weight_lo(STEP * t + u // 2 + 1, (u // 2 + 1) % STEP)

            rounds(0, True, False)
            with dve.Fori(1, ROUNDS - 1) as t:
                rounds(t, False, False)
            rounds(ROUNDS - 1, False, True)
            hidden_lo(UNITS * ROUNDS - 1, (UNITS - 1) % RING)
            dve.wait_ge(a_resT, 1)
            for j in range(2):
                dve.wait_ge(down_done, UNITS * ROUNDS - 1 + j)
                nc.vector.tensor_tensor(tC[:, hs(j)], half(6, j), tA[:, hs(j)], ALU.add).then_inc(fin_ready, 1)

        @block.tensor
        def _(pe):
            mm = nc.tensor.matmul
            pe.wait_ge(in_w, 16)
            for k in range(KCHUNKS):
                pe.wait_ge(in_patch[k], 16)
                for j in range(2):
                    ins = mm(half(0, j), wpat[:, k, :], pat[:, k, hs(j)], start=(k == 0), stop=(k == KCHUNKS - 1))
                    if k == KCHUNKS - 1:
                        ins.then_inc(p_embed, 1)
            pe.wait_ge(in_small, 80)
            for j in range(2):
                pe.wait_ge(v_x, j + 1)
                mm(half(2, j, CS), w_cs, tA[:, hs(j)], start=True, stop=True).then_inc(p_cs, 1)
            for j in range(2):
                pe.wait_ge(a_cs, 2 * j + 2)
                mm(half(4, j), embw[:, 0:DIM], cs_val[:, hs(j)], start=True, stop=True).then_inc(p_man, 1)
                mm(half(6, j), embw[:, DIM:], cs_sq[:, hs(j)], start=True, stop=True).then_inc(p_man, 1)
            pe.wait_ge(in_const, 64)
            for j in range(2):
                pe.wait_ge(v_enh, j + 1)
                mm(half(0, j), center, tC[:, hs(j)], start=True, stop=True).then_inc(p_center, 1)
            pe.wait_ge(v_prep, 2)
            pe.wait_ge(a_man, 2)
            mm(ps[0:PAIR, 5, 0:DIM], beta_bc[:], w_out, start=True, stop=True).then_inc(p_bias, 1)
            for c in range(PAIRS):
                pe.wait_ge(v_xc, c // QUAD + 1)
                mm(chunk(2, c), tA[:, pr(c)], w_og[:], start=True, stop=True)
                mm(ps[0:PAIR, 4, c:c + 1], tB[:, pr(c)], mean_col, start=True, stop=True).then_inc(p_h, 1)
            pe.wait_ge(v_norm, 1)
            for c in range(PAIRS):
                ins = nc.tensor.transpose(turned(6, c), n_tok[:, c, :], ident[0:PAIR, 0:PAIR])
                if c % QUAD == QUAD - 1:
                    ins.then_inc(p_turn1, 1)
            for j in range(2):
                pe.wait_ge(v_turn1 if j else a_turn1, 1)
                mm(half(0, j), w_q, tA[:, hs(j)], start=True, stop=True).then_inc(p_q, 1)
                mm(half(2, j), w_k, tA[:, hs(j)], start=True, stop=True).then_inc(p_k, 1)
                pe.wait_ge(v_var, 1)
                for c in range(j * QUAD, (j + 1) * QUAD):
                    ins = mm(chunk(4, c), tA[:, pr(c)], w_v, start=True, stop=True)
                ins.then_inc(p_v, 1)

            def scores(c):
                if c >= 3:
                    pe.wait_ge(v_mask, 2 * (c - 3) + 2)
                if c == 0:
                    pe.wait_ge(v_turn1, 1)
                    pe.wait_ge(v_prep, 3)
                    pe.wait_ge(a_q, 1 + HEADS // 2)
                    pe.wait_ge(a_k, 1)
                if c == 1:
                    pe.wait_ge(v_prep, 4)
                    pe.wait_ge(a_q, 1 + HEADS)
                    pe.wait_ge(a_k, 2)
                if c == 2:
                    pe.wait_ge(v_v, 2)
                w = HEADS // 2
                for g in range(2):
                    mm(ps[0:PAIR, SCORE_BANKS[c % 3] + g, 0:HALF], tB[:, pr(c)], q_blk[:, g * w:(g + 1) * w, pr(c)],
                       start=True, stop=True).then_inc(p_score, 1)

            def attend(c):
                pe.wait_ge(v_mask, 2 * c + 2)
                if c == 0:
                    pe.wait_ge(v_v, 2)
                    pe.wait_ge(a_k, 2)
                for h in range(HEADS):
                    ins = mm(chunk(2, c)[:, h * HD:(h + 1) * HD], attn[:, c % 2, h * PAIR:(h + 1) * PAIR],
                             v_tok[:, c, h * HD:(h + 1) * HD], start=True, stop=True)
                ins.then_inc(p_attn, 1)

            for c in range(PAIRS + 1):
                if c < PAIRS:
                    scores(c)
                if c:
                    attend(c - 1)
            groups = HEADS * PAIRS
            pe.wait_ge(v_gsum, 1)
            mm(ps[0:PAIR, 6, 0:groups], same_image, g_sum[:], start=True, stop=True).then_inc(p_gmean, 1)
            pe.wait_ge(v_gsum, 3)
            mm(ps[0:PAIR, 7, 0:groups], same_image, g_sum[:], start=True, stop=True).then_inc(p_gvar, 1)
            pe.wait_ge(v_norm, 2)
            for c in range(PAIRS):
                ins = nc.tensor.transpose(turned(6, c), n_tok[:, c, :], ident[0:PAIR, 0:PAIR])
                if c % QUAD == QUAD - 1:
                    ins.then_inc(p_turn2, 1)
            for c in range(PAIRS):
                pe.wait_ge(v_y2T, c // QUAD + 1)
                ins = mm(ps[0:PAIR, 4, c * EXPERTS:(c + 1) * EXPERTS], tB[:, pr(c)], w_router, start=True, stop=True)
            ins.then_inc(p_logit, 1)
            pe.wait_ge(g_res, 2)
            for c in range(PAIRS):
                ins = nc.tensor.transpose(turned(2, c), h_tok[:, c, :], ident[0:PAIR, 0:PAIR])
            ins.then_inc(p_resT, 1)

            def split_product(dst, hi, lo, x_hi_ap, x_lo_ap, start, stop):
                mm(dst, hi, x_hi_ap, start=start, stop=False, skip_group_check=True)
                mm(dst, hi, x_lo_ap, start=False, stop=False, skip_group_check=True)
                return mm(dst, lo, x_hi_ap, start=False, stop=stop, skip_group_check=True)

            def down(n, u, first, last):
                pe.wait_ge(hid_hi_ready, n + 1)
                pe.wait_ge(hid_lo_ready, n + 1)
                k, e = u % RING, u // 2
                split_product(half(6, u % 2), w_hi[:, e, 2 * DIM:], w_lo[:, e, 2 * DIM:], hid_hi[:, k, :],
                              hid_lo[:, k, :], first, last).then_inc(down_done, 1)

            def unit(n, u, t):
                k, e = u % RING, u // 2
                if u % 2 == 0:
                    pe.wait_ge(w_hi_ready, STEP * t + e + 1)
                    pe.wait_ge(w_lo_ready, STEP * t + e + 1)
                at_least(pe, silu_ready, n - RING + 1)
                split_product(ps[:, 2 * k, 0:HALF], w_hi[:, e, 0:DIM], w_lo[:, e, 0:DIM], x_hi[:, hs(u % 2)],
                              x_lo[:, hs(u % 2)], True, True).then_inc(gate_ready, 1)
                at_least(pe, gated_ready, n - RING + 1)
                split_product(ps[:, 2 * k + 1, 0:HALF], w_hi[:, e, DIM:2 * DIM], w_lo[:, e, DIM:2 * DIM],
                              x_hi[:, hs(u % 2)], x_lo[:, hs(u % 2)], True, True).then_inc(up_ready, 1)

            pe.wait_ge(a_xhi, 2)
            pe.wait_ge(v_xlo, 2)
            for u in range(UNITS):
                if u == 1:
                    pe.wait_ge(a_resT, 1)
                if u == 2:
                    pe.wait_ge(v_gate, 1)
                    for c in range(PAIRS):
                        ins = nc.tensor.transpose(turned(4, c, EXPERTS), gate[:, c, :], ident[0:PAIR, 0:PAIR])
                    ins.then_inc(p_gateT, 1)
                    pe.wait_ge(v_gateT, 1)
                unit(u, u, 0)
                if u >= LAG:
                    down(u - LAG, u - LAG, u - LAG < 2, False)
            with pe.Fori(1, ROUNDS) as t:
                for u in range(UNITS):
                    unit(UNITS * t + u, u, t)
                    down(UNITS * t + u - LAG, (u - LAG) % UNITS, False, False)
            for u in range(UNITS - LAG, UNITS):
                down(UNITS * (ROUNDS - 1) + u, u, False, True)


SCORE_BANKS = (6, 0, 4)
POOL_DECAY = (BITS - 1) + 2 + 3 * (BITS - 1)


def kernel(**inputs):
    import concourse.bacc as bacc
    from concourse.bass_utils import run_bass_kernel_spmd

    a = {k.replace("L0_", ""): np.asarray(v) for k, v in inputs.items()}
    c128, cpair = layout_constants()
    x = a["x"].reshape(BATCH, CHANNELS, GRID, PATCH, GRID, PATCH).transpose(1, 3, 5, 0, 2, 4)
    embed = np.zeros((CS, 2 * DIM), np.float32)
    embed[0:COORD, 0:DIM] = a["tok_W_embed"]
    embed[COORD:, DIM:] = 1.0
    gates_up = [np.concatenate([a["ffn_sWg"], a["ffn_Wg"]]), np.concatenate([a["ffn_sWu"], a["ffn_Wu"]]),
                np.concatenate([a["ffn_sWd"], a["ffn_Wd"]])]
    arrays = {
        "patches": x.reshape(KCHUNKS, 128, TOKENS).transpose(1, 0, 2),
        "w_patch": a["tok_W_patch"].reshape(KCHUNKS, 128, DIM).transpose(1, 0, 2),
        "pos": a["tok_pos_embed"][0].T,
        "cols": np.stack([a["tok_b_patch"], a["tok_b_embed"], a["tok_ln_gamma"], a["tok_ln_beta"], a["attn_bq"],
                          a["attn_bk"]], axis=1),
        "bias_cs": np.concatenate([a["tok_b_coord"], a["tok_b_spinor"]])[:, None],
        "rows": np.stack([a["tok_b_out"], a["attn_bv"], a["attn_gn_w"], a["attn_gn_b"]])[None],
        "small_w": np.concatenate([a["tok_W_coord"], a["tok_W_spinor"], a["tok_W_out"], a["attn_Wq"].T, a["attn_Wk"].T,
                                   a["attn_Wv"].T, a["ffn_Wr"]], axis=1),
        "embed_w": embed,
        "gamma": a["attn_gamma"].reshape(1, 1),
        "c128": c128,
        "cpair": cpair,
        "experts_w": np.concatenate(gates_up, axis=2).transpose(1, 0, 2),
    }
    nc = bacc.Bacc("TRN2", target_bir_lowering=False, num_devices=1)
    feed, args = {}, []
    for name, value in arrays.items():
        value = np.ascontiguousarray(value)
        feed[f"in_{name}"] = value
        args.append(nc.dram_tensor(f"in_{name}", value.shape, mybir.dt.from_np(value.dtype), kind="ExternalInput").ap())
    args.append(nc.dram_tensor("out_t", (DIM, TOKENS), F32, kind="ExternalOutput").ap())
    build(nc, *args)
    r = run_bass_kernel_spmd(nc, [feed], core_ids=[0])
    return np.ascontiguousarray(r.results[0]["out_t"].T).reshape(BATCH, SEQ, DIM)
```

```python
from contextlib import ExitStack

import numpy as np

import concourse.bass as bass
from concourse import mybir

ALU = mybir.AluOpType
ACT = mybir.ActivationFunctionType
AX = mybir.AxisListType
F32 = mybir.dt.float32
F32R = mybir.dt.float32r

BATCH, CHANNELS, IMG, PATCH = 16, 3, 112, 16
GRID = IMG // PATCH
SEQ = GRID * GRID
TOKENS = BATCH * SEQ
DIM = 128
PDIM = CHANNELS * PATCH * PATCH
KCHUNKS = PDIM // 128
COORD, SPINOR = 8, 4
CS = COORD + SPINOR
HEADS = 8
HD = DIM // HEADS
EXPERTS, SHARED, TOPK = 64, 2, 6
ALL_EXPERTS = EXPERTS + SHARED
EPS = 1e-5

PAIR = 2 * SEQ
PAIRS = TOKENS // PAIR
HALF = TOKENS // 2
QUAD = PAIRS // 2
BITS = 6
SENT = 8
WCOLS = 3 * DIM
STEP = 3
ROUNDS = ALL_EXPERTS // STEP
UNITS = 2 * STEP
RING = 3
LAG = 3
WLOADS = 6


def layout_constants():
    c128 = np.zeros((128, 128 + 128 + HEADS + 1), np.float32)
    c128[:, 0:128] = np.eye(128)
    c128[:, 128:256] = np.eye(128) - 1.0 / 128
    c128[:, 256:256 + HEADS] = np.arange(128)[:, None] // HD == np.arange(HEADS)[None, :]
    c128[:, 256 + HEADS] = 1.0 / 128
    tok = np.arange(PAIR)
    same = tok[:, None] // SEQ == tok[None, :] // SEQ
    diff = tok[None, :] - tok[:, None]
    keep = same & (diff >= 0)
    cpair = np.zeros((PAIR, PAIR + 2 * BITS * PAIR), np.float32)
    cpair[:, 0:PAIR] = same
    for b in range(BITS):
        bit = (np.maximum(diff, 0) >> b) & 1
        mask = keep if b == 0 else np.ones_like(keep)
        cpair[:, PAIR * (1 + b):PAIR * (2 + b)] = bit * mask
        cpair[:, PAIR * (1 + BITS + b):PAIR * (2 + BITS + b)] = (1 - bit) * mask
    return c128, cpair


def build(nc, patches, w_patch, pos, cols, bias_cs, rows, small_w, embed_w, gamma, c128_d, cpair_d,
          experts_w, out):
    with ExitStack() as ctx:
        def sb(name, shape, dt=F32):
            return ctx.enter_context(nc.sbuf_tensor(name, shape, dt))

        def sem(name):
            return ctx.enter_context(nc.semaphore(name))

        gates_dram = nc.dram_tensor("gates_dram", [ALL_EXPERTS, TOKENS], F32, kind="Internal").ap()

        raw_w = sb("raw_w", [128, ALL_EXPERTS, WCOLS])
        c128 = sb("c128", [128, 256 + HEADS + 1])
        cpair = sb("cpair", [PAIR, PAIR * (1 + 2 * BITS)])
        colv = sb("colv", [128, 6])
        csb = sb("csb", [CS, 1])
        rowv = sb("rowv", [PAIR, 4, DIM])
        smallw = sb("smallw", [128, CS + 4 * DIM + EXPERTS])
        embw = sb("embw", [CS, 2 * DIM])
        posT = sb("posT", [128, SEQ])
        gam = sb("gam", [PAIR, BITS])
        ident = c128[:, 0:128]
        center = c128[:, 128:256]
        head_mask = c128[:, 256:256 + HEADS]
        mean_col = c128[:, 256 + HEADS:257 + HEADS]
        same_image = cpair[:, 0:PAIR]
        b_patch, b_embed, ln_gamma, ln_beta, bq, bk = (colv[:, i:i + 1] for i in range(6))
        b_out, bv, gn_w, gn_b = (rowv[:, i, :] for i in range(4))
        w_cs = smallw[:, 0:CS]
        w_out, w_q, w_k, w_v = (smallw[:, CS + i * DIM:CS + (i + 1) * DIM] for i in range(4))
        w_router = smallw[:, CS + 4 * DIM:]

        big = sb("big", [128, 8 * TOKENS])
        pat = big[:, 0:KCHUNKS * TOKENS].rearrange("p (k t) -> p k t", k=KCHUNKS)
        wpat = big[:, KCHUNKS * TOKENS:KCHUNKS * TOKENS + PDIM].rearrange("p (k n) -> p k n", k=KCHUNKS)
        q_blk = big[:, :].rearrange("p (h t) -> p h t", h=HEADS)
        silu, gated = (big[:, i * RING * HALF:(i + 1) * RING * HALF].rearrange("p (r n) -> p r n", r=RING)
                       for i in range(2))

        tA = sb("tA", [128, TOKENS])
        tB = sb("tB", [128, TOKENS])
        tC = sb("tC", [128, TOKENS])
        w_og = sb("w_og", [128, DIM])
        beta_bc = sb("beta_bc", [128, PAIR])
        bq_mask = sb("bq_mask", [128, HEADS])
        h_tok = sb("h_tok", [PAIR, PAIRS, DIM])
        n_tok = sb("n_tok", [PAIR, PAIRS, DIM])
        v_tok = sb("v_tok", [PAIR, PAIRS, DIM])
        out_bias = sb("out_bias", [PAIR, DIM])
        decay = sb("decay", [PAIR, PAIR])
        dfac = sb("dfac", [PAIR, PAIR])
        attn = sb("attn", [PAIR, 2, HEADS * PAIR])
        cs_val, cs_sq = attn[0:CS, 0, :], attn[0:CS, 1, :]
        gateT = attn[0:EXPERTS, 0, :]
        stat = sb("stat", [PAIR, PAIRS, 6])
        mv = sb("mv", [PAIR, PAIRS, 2])
        r0 = sb("r0", [PAIR, PAIRS])
        rstd = sb("rstd", [PAIR, PAIRS])
        half_neg = sb("half_neg", [PAIR, PAIRS])
        g_sum = sb("g_sum", [PAIR, HEADS * PAIRS])
        g_mean = sb("g_mean", [PAIR, HEADS * PAIRS])
        g_rstd = sb("g_rstd", [PAIR, HEADS * PAIRS])
        prob = sb("prob", [PAIR, PAIRS, EXPERTS + SENT])
        gate = sb("gate", [PAIR, PAIRS, EXPERTS])
        repl = v_tok[:, :, :].rearrange("p c n -> p (c n)")[:, 0:PAIRS * (EXPERTS + SENT)].rearrange(
            "p (c n) -> p c n", c=PAIRS)
        top8 = sb("top8", [PAIR, PAIRS, 8])
        r_stat = sb("r_stat", [PAIR, 4, PAIRS])
        ones_row = sb("ones_row", [SHARED, TOKENS])
        x_hi = sb("x_hi", [128, TOKENS], F32R)
        x_lo = sb("x_lo", [128, TOKENS], F32R)
        w_hi = sb("w_hi", [128, STEP, WCOLS], F32R)
        w_lo = sb("w_lo", [128, STEP, WCOLS], F32R)
        gate_bc = sb("gate_bc", [128, STEP, TOKENS])
        hid_hi = sb("hid_hi", [128, RING, HALF], F32R)
        hid_lo = sb("hid_lo", [128, RING, HALF], F32R)

        ps = ctx.enter_context(nc.psum_tensor("ps", [128, 8, 512], F32))

        def half(bank, j, m=128):
            return ps[0:m, bank + j, 0:HALF]

        def both(bank, m=128):
            return ps[0:m, bank:bank + 2, 0:HALF]

        def chunk(bank, c, m=PAIR):
            return ps[0:m, bank + c // QUAD, (c % QUAD) * DIM:(c % QUAD + 1) * DIM]

        def chunks(bank, j):
            return ps[0:PAIR, bank + j, :].rearrange("p (c n) -> p c n", n=DIM)

        def turned(bank, c, m=128):
            return ps[0:m, bank + c // QUAD, (c % QUAD) * PAIR:(c % QUAD + 1) * PAIR]

        def cols2(t):
            return t[:, :].rearrange("p (j n) -> p j n", j=2)

        def hs(j):
            return slice(j * HALF, (j + 1) * HALF)

        def pr(c):
            return slice(c * PAIR, (c + 1) * PAIR)

        def over_dim(t):
            return t.unsqueeze(2).broadcast_to([PAIR, PAIRS, DIM])

        in_w = sem("in_w")
        in_patch = [sem(f"in_patch{k}") for k in range(KCHUNKS)]
        in_small = sem("in_small")
        in_const = sem("in_const")
        in_experts = sem("in_experts")
        ones_stored = sem("ones_stored")
        gates_stored = sem("gates_stored")
        gate_in = [sem(f"gate_in{k}") for k in range(STEP)]
        out_stored = sem("out_stored")
        p_embed = sem("p_embed")
        p_cs = sem("p_cs")
        p_man = sem("p_man")
        p_center = sem("p_center")
        p_bias = sem("p_bias")
        p_h = sem("p_h")
        p_turn1 = sem("p_turn1")
        p_q = sem("p_q")
        p_k = sem("p_k")
        p_v = sem("p_v")
        p_score = sem("p_score")
        p_attn = sem("p_attn")
        p_gmean = sem("p_gmean")
        p_gvar = sem("p_gvar")
        p_turn2 = sem("p_turn2")
        p_logit = sem("p_logit")
        p_resT = sem("p_resT")
        p_gateT = sem("p_gateT")
        a_cs = sem("a_cs")
        a_man = sem("a_man")
        a_sq = sem("a_sq")
        a_turn1 = sem("a_turn1")
        a_q = sem("a_q")
        a_k = sem("a_k")
        a_gmean = sem("a_gmean")
        a_gsq = sem("a_gsq")
        a_xhi = sem("a_xhi")
        a_exp = sem("a_exp")
        a_resT = sem("a_resT")
        g_prep = sem("g_prep")
        g_decay = sem("g_decay")
        g_pow = sem("g_pow")
        g_res = sem("g_res")
        v_prep = sem("v_prep")
        v_x = sem("v_x")
        v_enh = sem("v_enh")
        v_xc = sem("v_xc")
        v_bias = sem("v_bias")
        v_var = sem("v_var")
        v_norm = sem("v_norm")
        v_turn1 = sem("v_turn1")
        v_v = sem("v_v")
        v_mask = sem("v_mask")
        v_gsum = sem("v_gsum")
        v_cen = sem("v_cen")
        v_h2 = sem("v_h2")
        v_y2T = sem("v_y2T")
        v_xlo = sem("v_xlo")
        v_logit = sem("v_logit")
        v_gate = sem("v_gate")
        v_gateT = sem("v_gateT")
        dve_chain = sem("dve_chain")
        pool_chain = sem("pool_chain")
        gu_hi_ready = sem("gu_hi_ready")
        gu_lo_ready = sem("gu_lo_ready")
        dn_hi_ready = sem("dn_hi_ready")
        dn_lo_ready = sem("dn_lo_ready")
        gate_ready = sem("gate_ready")
        up_ready = sem("up_ready")
        silu_ready = sem("silu_ready")
        gated_ready = sem("gated_ready")
        hid_ready = sem("hid_ready")
        hid_hi_ready = sem("hid_hi_ready")
        hid_lo_ready = sem("hid_lo_ready")
        a_gsd = sem("a_gsd")
        v_gvar = sem("v_gvar")
        down_done = sem("down_done")
        fin_ready = sem("fin_ready")

        gu_cols, dn_cols = slice(0, 2 * DIM), slice(2 * DIM, WCOLS)

        def raw(e, cols):
            if isinstance(e, int):
                return raw_w[:, e, cols]
            return raw_w[:, bass.ds(e, 1), cols].rearrange("p o n -> p (o n)")

        block = ctx.enter_context(nc.Block())

        def at_least(eng, s, value):
            if isinstance(value, int) and value <= 0:
                return
            eng.wait_ge(s, value)

        @block.sync
        def _(sp):
            sp.dma_start(wpat, w_patch).then_inc(in_w, 16)
            for k in range(KCHUNKS):
                sp.dma_start(pat[:, k, :], patches[:, k, :]).then_inc(in_patch[k], 16)
                if k == 0:
                    sp.dma_start(colv[:], cols).then_inc(in_small, 16)
                    sp.dma_start(posT[:], pos).then_inc(in_small, 16)
                    sp.dma_start(csb[:], bias_cs).then_inc(in_small, 16)
                    sp.dma_start(smallw[:], small_w).then_inc(in_small, 16)
                    sp.dma_start(embw[:], embed_w).then_inc(in_small, 16)
            sp.dma_start(c128[:], c128_d).then_inc(in_const, 16)
            sp.dma_start(rowv[:], rows.broadcast_to([PAIR, 4, DIM])).then_inc(in_const, 16)
            sp.dma_start(gam[:, 0:1], gamma.broadcast_to([PAIR, 1])).then_inc(in_const, 16)
            sp.dma_start(cpair[:], cpair_d).then_inc(in_const, 16)
            n = ALL_EXPERTS // WLOADS
            for g in range(WLOADS):
                sp.dma_start(raw_w[:, g * n:(g + 1) * n, :], experts_w[:, g * n:(g + 1) * n, :]).then_inc(in_experts, 16)
            sp.wait_ge(g_prep, 1)
            sp.dma_start(gates_dram[0:SHARED, :], ones_row[:]).then_inc(ones_stored, 16)
            sp.wait_ge(ones_stored, 16)

            def load_gate(e, k):
                sp.dma_start(gate_bc[:, k, :], gates_dram[bass.ds(e, 1), :].broadcast_to([128, TOKENS])).then_inc(gate_in[k], 16)

            for e in range(SHARED):
                load_gate(e, e)
            sp.wait_ge(v_gateT, 1)
            sp.dma_start(gates_dram[SHARED:, :], gateT).then_inc(gates_stored, 16)
            sp.wait_ge(gates_stored, 16)
            for e in range(SHARED, STEP):
                load_gate(e, e)
            with sp.Fori(1, ROUNDS) as t:
                for k in range(STEP):
                    sp.wait_ge(gated_ready, UNITS * t - UNITS + 2 * k + 2)
                    load_gate(STEP * t + k, k)
            for j in range(2):
                sp.wait_ge(fin_ready, j + 1)
                sp.dma_start(out[:, hs(j)], tC[:, hs(j)]).then_inc(out_stored, 16)
            sp.wait_ge(out_stored, 32)

        @block.gpsimd
        def _(pool):
            steps = [0]

            def link(ins):
                steps[0] += 1
                ins.then_inc(pool_chain, 1)
                pool.wait_ge(pool_chain, steps[0])

            nc.gpsimd.memset(ones_row[:], 1.0).then_inc(g_prep, 1)
            nc.gpsimd.memset(half_neg[:], -0.5).then_inc(g_prep, 1)
            nc.gpsimd.memset(prob[:, :, EXPERTS:], -1.0).then_inc(g_prep, 1)
            pool.wait_ge(in_const, 64)
            for b in range(1, BITS):
                link(nc.gpsimd.tensor_tensor(gam[:, b:b + 1], gam[:, b - 1:b], gam[:, b - 1:b], ALU.mult))
            for b in range(BITS):
                bit = cpair[:, PAIR * (1 + b):PAIR * (2 + b)]
                nbit = cpair[:, PAIR * (1 + BITS + b):PAIR * (2 + BITS + b)]
                dst = decay[:] if b == 0 else dfac[:]
                link(nc.gpsimd.tensor_scalar(dst, bit, gam[:, b:b + 1], None, ALU.mult))
                link(nc.gpsimd.tensor_tensor(dst, dst, nbit, ALU.add))
                if b:
                    link(nc.gpsimd.tensor_tensor(decay[:], decay[:], dfac[:], ALU.mult))
            pool.wait_ge(g_prep, 3)

            def inverse_root(n, out_ap, in_ap):
                pool.wait_ge(v_var, n)
                nc.gpsimd.tensor_tensor(out_ap, in_ap, half_neg[:], ALU.pow).then_inc(g_pow, 1)

            for n in range(2):
                inverse_root(n + 1, rstd[:], r0[:])
            pool.wait_ge(v_norm, 1)
            nc.gpsimd.tensor_tensor(h_tok[:], h_tok[:], gn_b.unsqueeze(1).broadcast_to([PAIR, PAIRS, DIM]),
                                    ALU.add).then_inc(g_res, 1)
            inverse_root(3, rstd[:], r0[:])
            pool.wait_ge(v_norm, 2)
            nc.gpsimd.tensor_tensor(h_tok[:], h_tok[:], n_tok[:], ALU.add).then_inc(g_res, 1)

            def rounds(t):
                for u in range(UNITS):
                    n, k = UNITS * t + u, u % RING
                    pool.wait_ge(gate_in[u // 2], 16 * t + 16)
                    pool.wait_ge(silu_ready, n + 1)
                    at_least(pool, hid_ready, n - RING + 1)
                    nc.gpsimd.tensor_tensor(gated[:, k, :], silu[:, k, :], gate_bc[:, u // 2, hs(u % 2)],
                                            ALU.mult).then_inc(gated_ready, 1)

            rounds(0)
            with pool.Fori(1, ROUNDS) as t:
                rounds(t)

        @block.scalar
        def _(act):
            def copy(out_ap, in_ap, s):
                nc.scalar.activation(out_ap, in_ap, ACT.Copy).then_inc(s, 1)

            act.wait_ge(in_small, 80)
            for j in range(2):
                act.wait_ge(p_cs, j + 1)
                nc.scalar.activation(cs_val[:, hs(j)], half(2, j, CS), ACT.Identity, bias=csb[:, 0:1]).then_inc(a_cs, 1)
                nc.scalar.activation(cs_sq[:, hs(j)], half(2, j, CS), ACT.Square, bias=csb[:, 0:1]).then_inc(a_cs, 1)
            for j in range(2):
                act.wait_ge(p_man, 2 * j + 1)
                nc.scalar.activation(tB[:, hs(j)], half(4, j), ACT.Identity, bias=b_embed).then_inc(a_man, 1)
            for j in range(2):
                act.wait_ge(p_center, j + 1)
                if j == 0:
                    act.wait_ge(v_enh, 2)
                nc.scalar.activation(tB[:, hs(j)], half(0, j), ACT.Square).then_inc(a_sq, 1)
            act.wait_ge(in_const, 64)
            nc.scalar.activation(bq_mask[:], head_mask, ACT.Copy, scale=bq).then_inc(a_q, 1)
            act.wait_ge(p_turn1, 1)
            copy(tA[:, hs(0)], half(6, 0), a_turn1)
            act.wait_ge(a_q, 1)
            act.wait_ge(p_q, 1)
            for h in range(HEADS // 2):
                nc.scalar.activation(q_blk[:, h, hs(0)], half(0, 0), ACT.Identity, bias=bq_mask[:, h:h + 1],
                                     scale=head_mask[:, h:h + 1]).then_inc(a_q, 1)
            act.wait_ge(p_k, 1)
            nc.scalar.activation(tB[:, hs(0)], half(2, 0), ACT.Identity, bias=bk).then_inc(a_k, 1)
            act.wait_ge(p_q, 2)
            for h in range(HEADS // 2):
                nc.scalar.activation(q_blk[:, h, hs(1)], half(0, 1), ACT.Identity, bias=bq_mask[:, h:h + 1],
                                     scale=head_mask[:, h:h + 1]).then_inc(a_q, 1)
            act.wait_ge(p_k, 2)
            nc.scalar.activation(tB[:, hs(1)], half(2, 1), ACT.Identity, bias=bk).then_inc(a_k, 1)
            act.wait_ge(p_gmean, 1)
            nc.scalar.activation(g_mean[:], ps[0:PAIR, 6, 0:HEADS * PAIRS], ACT.Copy,
                                 scale=1.0 / (SEQ * HD)).then_inc(a_gmean, 1)
            for j in range(2):
                act.wait_ge(v_cen, j + 1)
                nc.scalar.activation(v_tok[:, j * QUAD:(j + 1) * QUAD, :], n_tok[:, j * QUAD:(j + 1) * QUAD, :],
                                     ACT.Square).then_inc(a_gsq, 1)
            act.wait_ge(v_gvar, 1)
            nc.scalar.activation(g_mean[:], g_sum[:], ACT.Sqrt).then_inc(a_gsd, 1)
            for j in range(2):
                act.wait_ge(p_turn2, j + 1)
                copy(x_hi[:, hs(j)], half(6, j), a_xhi)
            act.wait_ge(in_experts, 16 * WLOADS)

            def gate_up_hi(e, k):
                at_least(act, up_ready, 2 * e - 2 * STEP + 2)
                nc.scalar.activation(w_hi[:, k, gu_cols], raw(e, gu_cols), ACT.Copy).then_inc(gu_hi_ready, 1)

            def down_hi(e, k):
                at_least(act, down_done, 2 * e - 2 * STEP + 2)
                nc.scalar.activation(w_hi[:, k, dn_cols], raw(e, dn_cols), ACT.Copy).then_inc(dn_hi_ready, 1)

            gate_up_hi(0, 0)
            gate_up_hi(1, 1)
            act.wait_ge(v_logit, 1)
            nc.scalar.activation(prob[:, :, 0:EXPERTS], gate[:], ACT.Exp).then_inc(a_exp, 1)
            act.wait_ge(p_resT, 1)
            nc.scalar.activation(cols2(tA), both(2), ACT.Copy).then_inc(a_resT, 1)

            def hidden_hi(n, k):
                act.wait_ge(hid_ready, n + 1)
                at_least(act, down_done, n - RING + 1)
                nc.scalar.activation(hid_hi[:, k, :], ps[:, 2 * k + 1, 0:HALF], ACT.Copy).then_inc(hid_hi_ready, 1)

            def rounds(t, first, final):
                for u in range(UNITS):
                    n = UNITS * t + u
                    act.wait_ge(gate_ready, n + 1)
                    at_least(act, gated_ready, n - RING + 1)
                    nc.scalar.activation(silu[:, u % RING, :], ps[:, 2 * (u % RING), 0:HALF], ACT.Silu).then_inc(silu_ready, 1)
                    if not (first and u == 0):
                        hidden_hi(n - 1, (u - 1) % RING)
                    if u % 2 == 0:
                        down_hi(STEP * t + u // 2, u // 2)
                    elif not (final and u > UNITS - 5):
                        gate_up_hi(STEP * t + u // 2 + 2, (u // 2 + 2) % STEP)

            rounds(0, True, False)
            with act.Fori(1, ROUNDS - 1) as t:
                rounds(t, False, False)
            rounds(ROUNDS - 1, False, True)
            hidden_hi(UNITS * ROUNDS - 1, (UNITS - 1) % RING)

        @block.vector
        def _(dve):
            steps = [0]

            def link(ins):
                steps[0] += 1
                ins.then_inc(dve_chain, 1)
                dve.wait_ge(dve_chain, steps[0])

            dve.wait_ge(in_small, 80)
            nc.vector.tensor_scalar(w_og[:], w_out, ln_gamma, None, ALU.mult).then_inc(v_prep, 1)
            nc.vector.tensor_copy(beta_bc[:], ln_beta.broadcast_to([128, PAIR])).then_inc(v_prep, 1)
            for j in range(2):
                dve.wait_ge(p_embed, j + 1)
                nc.vector.scalar_tensor_tensor(
                    out=tA[:, hs(j)].rearrange("p (b s) -> p b s", s=SEQ),
                    in0=half(0, j).rearrange("p (b s) -> p b s", s=SEQ), scalar=b_patch,
                    in1=posT[:].unsqueeze(1).broadcast_to([128, BATCH // 2, SEQ]),
                    op0=ALU.add, op1=ALU.add).then_inc(v_x, 1)
            for j in range(2):
                dve.wait_ge(a_man, j + 1)
                dve.wait_ge(p_man, 2 * j + 2)
                link(nc.vector.tensor_tensor(tC[:, hs(j)], half(6, j), tB[:, hs(j)], ALU.mult))
                nc.vector.tensor_tensor(tC[:, hs(j)], tC[:, hs(j)], tA[:, hs(j)], ALU.add).then_inc(v_enh, 1)
            for j in range(2):
                dve.wait_ge(p_center, j + 1)
                if j == 0:
                    dve.wait_ge(a_sq, 1)
                else:
                    dve.wait_ge(a_sq, 2)
                nc.vector.tensor_copy(tA[:, hs(j)], half(0, j)).then_inc(v_xc, 1)
            dve.wait_ge(in_const, 64)
            dve.wait_ge(p_bias, 1)
            nc.vector.tensor_tensor(out_bias[:], ps[0:PAIR, 5, 0:DIM], b_out, ALU.add).then_inc(v_bias, 1)
            dve.wait_ge(p_h, PAIRS)
            nc.vector.tensor_scalar(r0[:], ps[0:PAIR, 4, 0:PAIRS], EPS, None, ALU.add).then_inc(v_var, 1)
            dve.wait_ge(g_pow, 1)
            dve.wait_ge(v_bias, 1)

            def row_stats(make):
                for c in range(PAIRS):
                    if make:
                        make(c)
                for c in range(PAIRS):
                    last = nc.vector.bn_stats(stat[:, c, :], h_tok[:, c, :])
                link(last)
                for c in range(PAIRS):
                    last = nc.vector.bn_aggr(mv[:, c, :], stat[:, c, :])
                link(last)
                nc.vector.tensor_scalar(r0[:], mv[:, :, 1], EPS, None, ALU.add).then_inc(v_var, 1)

            def row_norm(s):
                for c in range(PAIRS):
                    last = nc.vector.tensor_scalar(n_tok[:, c, :], h_tok[:, c, :], mv[:, c, 0:1], rstd[:, c:c + 1],
                                                   ALU.subtract, ALU.mult)
                last.then_inc(s, 1)

            def make_h(c):
                ins = nc.vector.scalar_tensor_tensor(out=h_tok[:, c, :], in0=chunk(2, c), scalar=rstd[:, c:c + 1],
                                                     in1=out_bias[:], op0=ALU.mult, op1=ALU.add)
                if c == PAIRS - 1:
                    link(ins)

            row_stats(make_h)
            dve.wait_ge(g_pow, 2)
            row_norm(v_norm)
            dve.wait_ge(p_turn1, 2)
            nc.vector.tensor_copy(tA[:, hs(1)], half(6, 1)).then_inc(v_turn1, 1)
            dve.wait_ge(a_q, 1)
            for j in range(2):
                dve.wait_ge(p_q, j + 1)
                dve.wait_ge(a_q, 1 + HEADS // 2 * (j + 1))
                for h in range(HEADS // 2, HEADS):
                    ins = nc.vector.tensor_scalar(q_blk[:, h, hs(j)], half(0, j), head_mask[:, h:h + 1],
                                                  bq_mask[:, h:h + 1], ALU.mult, ALU.add)
                ins.then_inc(v_prep, 1)
            for j in range(2):
                dve.wait_ge(p_v, j + 1)
                nc.vector.tensor_tensor(v_tok[:, j * QUAD:(j + 1) * QUAD, :], chunks(4, j),
                                        bv.unsqueeze(1).broadcast_to([PAIR, QUAD, DIM]), ALU.add).then_inc(v_v, 1)
            dve.wait_ge(pool_chain, POOL_DECAY)
            for c in range(PAIRS):
                for g in range(2):
                    dve.wait_ge(p_score, 2 * c + g + 1)
                    if c >= 2:
                        dve.wait_ge(p_attn, c - 1)
                    bank = SCORE_BANKS[c % 3] + g
                    w = HEADS // 2
                    nc.vector.tensor_tensor(
                        attn[:, c % 2, g * HALF:(g + 1) * HALF].rearrange("p (h q) -> p h q", h=w),
                        ps[0:PAIR, bank, 0:HALF].rearrange("p (h q) -> p h q", h=w),
                        decay[:].unsqueeze(1).broadcast_to([PAIR, w, PAIR]), ALU.mult).then_inc(v_mask, 1)
            groups = HEADS * PAIRS

            def by_head(ap):
                return ap.rearrange("p c (h d) -> p (c h) d", d=HD)

            attn_out = ps[0:PAIR, 2:4, :].rearrange("p b (g d) -> p (b g) d", d=HD)
            dve.wait_ge(p_attn, PAIRS)
            nc.vector.tensor_reduce(g_sum[:], attn_out, AX.X, ALU.add).then_inc(v_gsum, 1)
            dve.wait_ge(a_gmean, 1)
            gh = groups // 2
            for j in range(2):
                nc.vector.tensor_tensor(by_head(n_tok[:, j * QUAD:(j + 1) * QUAD, :]), attn_out[:, j * gh:(j + 1) * gh, :],
                                        g_mean[:, j * gh:(j + 1) * gh].unsqueeze(2).broadcast_to([PAIR, gh, HD]),
                                        ALU.subtract).then_inc(v_cen, 1)
            weighted = attn[:, :, :].rearrange("p a n -> p (a n)")[:, 0:PAIRS * DIM].rearrange("p (c n) -> p c n", c=PAIRS)
            dve.wait_ge(v_cen, 2)
            nc.vector.tensor_tensor(weighted, n_tok[:], gn_w.unsqueeze(1).broadcast_to([PAIR, PAIRS, DIM]),
                                    ALU.mult).then_inc(v_cen, 1)
            for j in range(2):
                dve.wait_ge(a_gsq, j + 1)
                nc.vector.tensor_reduce(g_sum[:, j * gh:(j + 1) * gh], by_head(v_tok[:, j * QUAD:(j + 1) * QUAD, :]),
                                        AX.X, ALU.add).then_inc(v_gsum, 1)
            dve.wait_ge(p_gvar, 1)
            nc.vector.tensor_scalar(g_sum[:], ps[0:PAIR, 7, 0:groups], 1.0 / (SEQ * HD), EPS,
                                    ALU.mult, ALU.add).then_inc(v_gvar, 1)
            dve.wait_ge(a_gsd, 1)
            link(nc.vector.reciprocal(g_rstd[:], g_mean[:]))
            link(nc.vector.tensor_tensor(g_mean[:], g_rstd[:], g_rstd[:], ALU.mult))
            link(nc.vector.scalar_tensor_tensor(out=g_mean[:], in0=g_mean[:], scalar=-0.5, in1=g_sum[:],
                                                op0=ALU.mult, op1=ALU.mult))
            link(nc.vector.scalar_tensor_tensor(out=g_rstd[:], in0=g_mean[:], scalar=1.5, in1=g_rstd[:],
                                                op0=ALU.add, op1=ALU.mult))
            dve.wait_ge(v_cen, 3)
            dve.wait_ge(g_res, 1)
            link(nc.vector.tensor_tensor(by_head(weighted), by_head(weighted),
                                         g_rstd[:].unsqueeze(2).broadcast_to([PAIR, groups, HD]), ALU.mult))
            link(nc.vector.tensor_tensor(h_tok[:], h_tok[:], weighted, ALU.add))
            row_stats(None)
            dve.wait_ge(g_pow, 3)
            row_norm(v_norm)
            for j in range(2):
                dve.wait_ge(p_turn2, j + 1)
                dve.wait_ge(a_xhi, j + 1)
                nc.vector.tensor_copy(tB[:, hs(j)], half(6, j)).then_inc(v_y2T, 1)
            for j in range(2):
                nc.vector.tensor_tensor(x_lo[:, hs(j)], half(6, j), x_hi[:, hs(j)].bitcast(F32),
                                        ALU.subtract).then_inc(v_xlo, 1)
            def gate_up_lo(e, k):
                dve.wait_ge(gu_hi_ready, e + 1)
                at_least(dve, up_ready, 2 * e - 2 * STEP + 2)
                nc.vector.tensor_tensor(w_lo[:, k, gu_cols], raw(e, gu_cols), w_hi[:, k, gu_cols].bitcast(F32),
                                        ALU.subtract).then_inc(gu_lo_ready, 1)

            def down_lo(e, k):
                dve.wait_ge(dn_hi_ready, e + 1)
                at_least(dve, down_done, 2 * e - 2 * STEP + 2)
                nc.vector.tensor_tensor(w_lo[:, k, dn_cols], raw(e, dn_cols), w_hi[:, k, dn_cols].bitcast(F32),
                                        ALU.subtract).then_inc(dn_lo_ready, 1)

            gate_up_lo(0, 0)
            gate_up_lo(1, 1)
            logits = ps[0:PAIR, 4, :].rearrange("p (c e) -> p c e", e=EXPERTS)
            over_experts = [PAIR, PAIRS, EXPERTS]
            probs = prob[:, :, 0:EXPERTS]
            dve.wait_ge(p_logit, 1)
            link(nc.vector.tensor_reduce(r_stat[:, 0, :], logits, AX.X, ALU.max))
            nc.vector.tensor_tensor(gate[:], logits, r_stat[:, 0, :].unsqueeze(2).broadcast_to(over_experts),
                                    ALU.subtract).then_inc(v_logit, 1)
            dve.wait_ge(a_exp, 1)
            link(nc.vector.tensor_reduce(r_stat[:, 1, :], probs, AX.X, ALU.add))
            link(nc.vector.reciprocal(r_stat[:, 2, :], r_stat[:, 1, :]))
            dve.wait_ge(g_prep, 3)
            link(nc.vector.tensor_tensor(probs, probs, r_stat[:, 2, :].unsqueeze(2).broadcast_to(over_experts), ALU.mult))
            for c in range(PAIRS):
                last = nc.vector.max(top8[:, c, :], prob[:, c, :])
            link(last)
            link(nc.vector.memset(top8[:, :, TOPK:], -1.0))
            for c in range(PAIRS):
                last = nc.vector.match_replace(repl[:, c, :], top8[:, c, :], prob[:, c, :], -2.0)
            link(last)
            link(nc.vector.tensor_reduce(r_stat[:, 0, :], top8[:, :, 0:TOPK], AX.X, ALU.add))
            link(nc.vector.reciprocal(r_stat[:, 3, :], r_stat[:, 0, :]))
            link(nc.vector.scalar_tensor_tensor(out=gate[:], in0=repl[:, :, 0:EXPERTS], scalar=-1.5, in1=probs,
                                                op0=ALU.is_lt, op1=ALU.mult))
            nc.vector.tensor_tensor(gate[:], gate[:], r_stat[:, 3, :].unsqueeze(2).broadcast_to(over_experts),
                                    ALU.mult).then_inc(v_gate, 1)
            dve.wait_ge(p_gateT, 1)
            nc.vector.tensor_copy(cols2(gateT), both(4, EXPERTS)).then_inc(v_gateT, 1)

            def hidden_lo(n, k):
                dve.wait_ge(hid_hi_ready, n + 1)
                at_least(dve, down_done, n - RING + 1)
                nc.vector.tensor_tensor(hid_lo[:, k, :], ps[:, 2 * k + 1, 0:HALF], hid_hi[:, k, :].bitcast(F32),
                                        ALU.subtract).then_inc(hid_lo_ready, 1)

            def rounds(t, first, final):
                for u in range(UNITS):
                    n, k = UNITS * t + u, u % RING
                    dve.wait_ge(gated_ready, n + 1)
                    dve.wait_ge(up_ready, n + 1)
                    up = ps[:, 2 * k + 1, 0:HALF]
                    nc.vector.tensor_tensor(up, up, gated[:, k, :], ALU.mult).then_inc(hid_ready, 1)
                    if not (first and u == 0):
                        hidden_lo(n - 1, (u - 1) % RING)
                    if u % 2 == 0:
                        down_lo(STEP * t + u // 2, u // 2)
                    elif not (final and u > UNITS - 5):
                        gate_up_lo(STEP * t + u // 2 + 2, (u // 2 + 2) % STEP)

            rounds(0, True, False)
            with dve.Fori(1, ROUNDS - 1) as t:
                rounds(t, False, False)
            rounds(ROUNDS - 1, False, True)
            hidden_lo(UNITS * ROUNDS - 1, (UNITS - 1) % RING)
            dve.wait_ge(a_resT, 1)
            for j in range(2):
                dve.wait_ge(down_done, UNITS * ROUNDS - 1 + j)
                nc.vector.tensor_tensor(tC[:, hs(j)], half(6, j), tA[:, hs(j)], ALU.add).then_inc(fin_ready, 1)

        @block.tensor
        def _(pe):
            mm = nc.tensor.matmul
            pe.wait_ge(in_w, 16)
            for k in range(KCHUNKS):
                pe.wait_ge(in_patch[k], 16)
                for j in range(2):
                    ins = mm(half(0, j), wpat[:, k, :], pat[:, k, hs(j)], start=(k == 0), stop=(k == KCHUNKS - 1))
                    if k == KCHUNKS - 1:
                        ins.then_inc(p_embed, 1)
            pe.wait_ge(in_small, 80)
            for j in range(2):
                pe.wait_ge(v_x, j + 1)
                mm(half(2, j, CS), w_cs, tA[:, hs(j)], start=True, stop=True).then_inc(p_cs, 1)
            for j in range(2):
                pe.wait_ge(a_cs, 2 * j + 2)
                mm(half(4, j), embw[:, 0:DIM], cs_val[:, hs(j)], start=True, stop=True).then_inc(p_man, 1)
                mm(half(6, j), embw[:, DIM:], cs_sq[:, hs(j)], start=True, stop=True).then_inc(p_man, 1)
            pe.wait_ge(in_const, 64)
            for j in range(2):
                pe.wait_ge(v_enh, j + 1)
                mm(half(0, j), center, tC[:, hs(j)], start=True, stop=True).then_inc(p_center, 1)
            pe.wait_ge(v_prep, 2)
            pe.wait_ge(a_man, 2)
            mm(ps[0:PAIR, 5, 0:DIM], beta_bc[:], w_out, start=True, stop=True).then_inc(p_bias, 1)
            for c in range(PAIRS):
                pe.wait_ge(v_xc, c // QUAD + 1)
                mm(chunk(2, c), tA[:, pr(c)], w_og[:], start=True, stop=True)
                mm(ps[0:PAIR, 4, c:c + 1], tB[:, pr(c)], mean_col, start=True, stop=True).then_inc(p_h, 1)
            pe.wait_ge(v_norm, 1)
            for c in range(PAIRS):
                ins = nc.tensor.transpose(turned(6, c), n_tok[:, c, :], ident[0:PAIR, 0:PAIR])
                if c % QUAD == QUAD - 1:
                    ins.then_inc(p_turn1, 1)
            for j in range(2):
                pe.wait_ge(v_turn1 if j else a_turn1, 1)
                mm(half(0, j), w_q, tA[:, hs(j)], start=True, stop=True).then_inc(p_q, 1)
                mm(half(2, j), w_k, tA[:, hs(j)], start=True, stop=True).then_inc(p_k, 1)
                pe.wait_ge(v_var, 1)
                for c in range(j * QUAD, (j + 1) * QUAD):
                    ins = mm(chunk(4, c), tA[:, pr(c)], w_v, start=True, stop=True)
                ins.then_inc(p_v, 1)

            def scores(c):
                if c >= 3:
                    pe.wait_ge(v_mask, 2 * (c - 3) + 2)
                if c == 0:
                    pe.wait_ge(v_turn1, 1)
                    pe.wait_ge(v_prep, 3)
                    pe.wait_ge(a_q, 1 + HEADS // 2)
                    pe.wait_ge(a_k, 1)
                if c == 1:
                    pe.wait_ge(v_prep, 4)
                    pe.wait_ge(a_q, 1 + HEADS)
                    pe.wait_ge(a_k, 2)
                if c == 2:
                    pe.wait_ge(v_v, 2)
                w = HEADS // 2
                for g in range(2):
                    mm(ps[0:PAIR, SCORE_BANKS[c % 3] + g, 0:HALF], tB[:, pr(c)], q_blk[:, g * w:(g + 1) * w, pr(c)],
                       start=True, stop=True).then_inc(p_score, 1)

            def attend(c):
                pe.wait_ge(v_mask, 2 * c + 2)
                if c == 0:
                    pe.wait_ge(v_v, 2)
                    pe.wait_ge(a_k, 2)
                for h in range(HEADS):
                    ins = mm(chunk(2, c)[:, h * HD:(h + 1) * HD], attn[:, c % 2, h * PAIR:(h + 1) * PAIR],
                             v_tok[:, c, h * HD:(h + 1) * HD], start=True, stop=True)
                ins.then_inc(p_attn, 1)

            for c in range(PAIRS + 1):
                if c < PAIRS:
                    scores(c)
                if c:
                    attend(c - 1)
            groups = HEADS * PAIRS
            pe.wait_ge(v_gsum, 1)
            mm(ps[0:PAIR, 6, 0:groups], same_image, g_sum[:], start=True, stop=True).then_inc(p_gmean, 1)
            pe.wait_ge(v_gsum, 3)
            mm(ps[0:PAIR, 7, 0:groups], same_image, g_sum[:], start=True, stop=True).then_inc(p_gvar, 1)
            pe.wait_ge(v_norm, 2)
            for c in range(PAIRS):
                ins = nc.tensor.transpose(turned(6, c), n_tok[:, c, :], ident[0:PAIR, 0:PAIR])
                if c % QUAD == QUAD - 1:
                    ins.then_inc(p_turn2, 1)
            for c in range(PAIRS):
                pe.wait_ge(v_y2T, c // QUAD + 1)
                ins = mm(ps[0:PAIR, 4, c * EXPERTS:(c + 1) * EXPERTS], tB[:, pr(c)], w_router, start=True, stop=True)
            ins.then_inc(p_logit, 1)
            pe.wait_ge(g_res, 2)
            for c in range(PAIRS):
                ins = nc.tensor.transpose(turned(2, c), h_tok[:, c, :], ident[0:PAIR, 0:PAIR])
            ins.then_inc(p_resT, 1)

            def split_product(dst, hi, lo, x_hi_ap, x_lo_ap, start, stop):
                mm(dst, hi, x_hi_ap, start=start, stop=False, skip_group_check=True)
                mm(dst, hi, x_lo_ap, start=False, stop=False, skip_group_check=True)
                return mm(dst, lo, x_hi_ap, start=False, stop=stop, skip_group_check=True)

            def down(t, u, first, last):
                n = UNITS * t + u
                pe.wait_ge(hid_hi_ready, n + 1)
                pe.wait_ge(hid_lo_ready, n + 1)
                k, e = u % RING, u // 2
                if u % 2 == 0:
                    pe.wait_ge(dn_hi_ready, STEP * t + e + 1)
                    pe.wait_ge(dn_lo_ready, STEP * t + e + 1)
                split_product(half(6, u % 2), w_hi[:, e, 2 * DIM:], w_lo[:, e, 2 * DIM:], hid_hi[:, k, :],
                              hid_lo[:, k, :], first, last).then_inc(down_done, 1)

            def unit(t, u, between):
                n, k, e = UNITS * t + u, u % RING, u // 2
                if u % 2 == 0:
                    pe.wait_ge(gu_hi_ready, STEP * t + e + 1)
                    pe.wait_ge(gu_lo_ready, STEP * t + e + 1)
                at_least(pe, silu_ready, n - RING + 1)
                split_product(ps[:, 2 * k, 0:HALF], w_hi[:, e, 0:DIM], w_lo[:, e, 0:DIM], x_hi[:, hs(u % 2)],
                              x_lo[:, hs(u % 2)], True, True).then_inc(gate_ready, 1)
                if between:
                    down(*between)
                at_least(pe, hid_lo_ready, n - RING + 1)
                split_product(ps[:, 2 * k + 1, 0:HALF], w_hi[:, e, DIM:2 * DIM], w_lo[:, e, DIM:2 * DIM],
                              x_hi[:, hs(u % 2)], x_lo[:, hs(u % 2)], True, True).then_inc(up_ready, 1)

            pe.wait_ge(a_xhi, 2)
            pe.wait_ge(v_xlo, 2)
            for u in range(UNITS):
                if u == 1:
                    pe.wait_ge(a_resT, 1)
                if u == 2:
                    pe.wait_ge(v_gate, 1)
                    for c in range(PAIRS):
                        ins = nc.tensor.transpose(turned(4, c, EXPERTS), gate[:, c, :], ident[0:PAIR, 0:PAIR])
                    ins.then_inc(p_gateT, 1)
                    pe.wait_ge(v_gateT, 1)
                unit(0, u, (0, u - LAG, u - LAG < 2, False) if u >= LAG else None)
            with pe.Fori(1, ROUNDS) as t:
                for u in range(UNITS):
                    unit(t, u, (t - 1, UNITS + u - LAG, False, False) if u < LAG else (t, u - LAG, False, False))
            for u in range(UNITS - LAG, UNITS):
                down(ROUNDS - 1, u, False, True)


SCORE_BANKS = (6, 0, 4)
POOL_DECAY = (BITS - 1) + 2 + 3 * (BITS - 1)


def kernel(**inputs):
    import concourse.bacc as bacc
    from concourse.bass_utils import run_bass_kernel_spmd

    a = {k.replace("L0_", ""): np.asarray(v) for k, v in inputs.items()}
    c128, cpair = layout_constants()
    x = a["x"].reshape(BATCH, CHANNELS, GRID, PATCH, GRID, PATCH).transpose(1, 3, 5, 0, 2, 4)
    embed = np.zeros((CS, 2 * DIM), np.float32)
    embed[0:COORD, 0:DIM] = a["tok_W_embed"]
    embed[COORD:, DIM:] = 1.0
    gates_up = [np.concatenate([a["ffn_sWg"], a["ffn_Wg"]]), np.concatenate([a["ffn_sWu"], a["ffn_Wu"]]),
                np.concatenate([a["ffn_sWd"], a["ffn_Wd"]])]
    arrays = {
        "patches": x.reshape(KCHUNKS, 128, TOKENS).transpose(1, 0, 2),
        "w_patch": a["tok_W_patch"].reshape(KCHUNKS, 128, DIM).transpose(1, 0, 2),
        "pos": a["tok_pos_embed"][0].T,
        "cols": np.stack([a["tok_b_patch"], a["tok_b_embed"], a["tok_ln_gamma"], a["tok_ln_beta"], a["attn_bq"],
                          a["attn_bk"]], axis=1),
        "bias_cs": np.concatenate([a["tok_b_coord"], a["tok_b_spinor"]])[:, None],
        "rows": np.stack([a["tok_b_out"], a["attn_bv"], a["attn_gn_w"], a["attn_gn_b"]])[None],
        "small_w": np.concatenate([a["tok_W_coord"], a["tok_W_spinor"], a["tok_W_out"], a["attn_Wq"].T, a["attn_Wk"].T,
                                   a["attn_Wv"].T, a["ffn_Wr"]], axis=1),
        "embed_w": embed,
        "gamma": a["attn_gamma"].reshape(1, 1),
        "c128": c128,
        "cpair": cpair,
        "experts_w": np.concatenate(gates_up, axis=2).transpose(1, 0, 2),
    }
    nc = bacc.Bacc("TRN2", target_bir_lowering=False, num_devices=1)
    feed, args = {}, []
    for name, value in arrays.items():
        value = np.ascontiguousarray(value)
        feed[f"in_{name}"] = value
        args.append(nc.dram_tensor(f"in_{name}", value.shape, mybir.dt.from_np(value.dtype), kind="ExternalInput").ap())
    args.append(nc.dram_tensor("out_t", (DIM, TOKENS), F32, kind="ExternalOutput").ap())
    build(nc, *args)
    r = run_bass_kernel_spmd(nc, [feed], core_ids=[0])
    return np.ascontiguousarray(r.results[0]["out_t"].T).reshape(BATCH, SEQ, DIM)
```
